# Optimizing a Trainium2 kernel written in Bass

```python
import numpy as np
import jax
import jax.numpy as jnp

def _softmax(x, axis=-1):
    return jax.nn.softmax(x, axis=axis)

def _gelu(x):
    return jax.nn.gelu(x, approximate=True)

def _silu(x):
    return jax.nn.silu(x)

def _sigmoid(x):
    return jax.nn.sigmoid(x)

def _layernorm(x, axis=-1, eps=1e-05):
    m = jnp.mean(x, axis=axis, keepdims=True)
    v = jnp.var(x, axis=axis, keepdims=True)
    return (x - m) / jnp.sqrt(v + eps)

def _scatter_add(tgt, idx, src, axis=0):
    return tgt.at[idx].add(src)

def _segment_sum(src, seg, n):
    return jax.ops.segment_sum(src, seg, n)
kernel_name = 'mk_xattn_seq_d1_seqx_r2_4d67ff'

def setup_inputs(seed: int=0):
    np.random.seed(seed)
    _w = jnp.asarray

    def _rec_inputs():
        import jax
        import jax.numpy as jnp
        _rk = jax.random.key(seed)
        x = -0.0002928 + 1 * jax.random.normal(jax.random.fold_in(_rk, 1), (8, 224, 512), jnp.float32)
        _lenS = 224 - jax.random.randint(jax.random.fold_in(_rk, 7), (8,), 0, max(1, 224 // 4) + 1, jnp.int32)
        _lenS2 = 750 - jax.random.randint(jax.random.fold_in(_rk, 8), (8,), 0, max(1, 750 // 4) + 1, jnp.int32)
        _ctx_1024P = jax.random.normal(jax.random.fold_in(_rk, 11), (8, 16, 512), jnp.float32)
        _ctx_1024c = jax.random.dirichlet(jax.random.fold_in(_rk, 511), 0.3 * jnp.ones((16,), jnp.float32), (8, 750))
        _ctx_1024t = jnp.einsum('bsk,bkd->bsd', _ctx_1024c, _ctx_1024P)
        _ctx_1024t = _ctx_1024t * jax.lax.rsqrt(jnp.mean(jnp.square(_ctx_1024t)) + 1e-12) * 0.953939
        ctx_1024 = -1.39393e-06 + 0.999914 * (_ctx_1024t + 0.3 * jax.random.normal(jax.random.fold_in(_rk, 611), (8, 750, 512), jnp.float32))
        return (x, ctx_1024)
    x, ctx_1024 = _rec_inputs()

    def _L0_xattn_setup():
        import jax, jax.numpy as jnp
        import numpy as np
        D_MODEL = 512
        HEADS = 16
        D_K = D_MODEL // HEADS
        key = jax.random.key(seed)
        ks = jax.random.split(key, 12)
        B, S = (2, 1024)
        s = 1.0 / np.sqrt(D_MODEL)
        return {'queries': jax.random.normal(ks[0], (B, S, D_MODEL), jnp.float32), 'keys': jax.random.normal(ks[1], (B, S, D_MODEL), jnp.float32), 'values': jax.random.normal(ks[2], (B, S, D_MODEL), jnp.float32), 'Wq': jax.random.normal(ks[3], (D_MODEL, D_MODEL), jnp.float32) * s, 'bq': jnp.zeros((D_MODEL,), jnp.float32), 'Wk': jax.random.normal(ks[4], (D_MODEL, D_MODEL), jnp.float32) * s, 'bk': jnp.zeros((D_MODEL,), jnp.float32), 'Wv': jax.random.normal(ks[5], (D_MODEL, D_MODEL), jnp.float32) * s, 'bv': jnp.zeros((D_MODEL,), jnp.float32), 'Wo': jax.random.normal(ks[6], (D_MODEL, D_MODEL), jnp.float32) * s, 'bo': jnp.zeros((D_MODEL,), jnp.float32), 'gamma': jnp.ones((D_MODEL,), jnp.float32), 'beta': jnp.zeros((D_MODEL,), jnp.float32)}
    _L0_xattn_all = _L0_xattn_setup()
    _L0_xattn_in = {k: v for k, v in _L0_xattn_all.items() if k in ('Wq', 'bq', 'Wk', 'bk', 'Wv', 'bv', 'Wo', 'bo', 'gamma', 'beta')}
    del _L0_xattn_all
    return {'x': x, 'ctx_1024': ctx_1024, 'L0_xattn_Wq': _L0_xattn_in['Wq'], 'L0_xattn_bq': _L0_xattn_in['bq'], 'L0_xattn_Wk': _L0_xattn_in['Wk'], 'L0_xattn_bk': _L0_xattn_in['bk'], 'L0_xattn_Wv': _L0_xattn_in['Wv'], 'L0_xattn_bv': _L0_xattn_in['bv'], 'L0_xattn_Wo': _L0_xattn_in['Wo'], 'L0_xattn_bo': _L0_xattn_in['bo'], 'L0_xattn_gamma': _L0_xattn_in['gamma'], 'L0_xattn_beta': _L0_xattn_in['beta']}

def reference(x, ctx_1024, L0_xattn_Wq, L0_xattn_bq, L0_xattn_Wk, L0_xattn_bk, L0_xattn_Wv, L0_xattn_bv, L0_xattn_Wo, L0_xattn_bo, L0_xattn_gamma, L0_xattn_beta):
    import jax
    import jax.numpy as jnp

    def _L0_xattn_ref(queries, keys, values, Wq, bq, Wk, bk, Wv, bv, Wo, bo, gamma, beta):
        import jax, jax.numpy as jnp
        import numpy as np
        D_MODEL = 512
        HEADS = 16
        D_K = D_MODEL // HEADS
        B, Nq, D = queries.shape
        Nk = keys.shape[1]
        q = (queries @ Wq.T + bq).reshape(B, Nq, HEADS, D_K).transpose(0, 2, 1, 3)
        k = (keys @ Wk.T + bk).reshape(B, Nk, HEADS, D_K).transpose(0, 2, 1, 3)
        v = (values @ Wv.T + bv).reshape(B, Nk, HEADS, D_K).transpose(0, 2, 1, 3)
        att = jnp.einsum('bhqd,bhkd->bhqk', q, k) / np.sqrt(D_K).astype(np.float32)
        att = jax.nn.softmax(att, axis=-1)
        out = jnp.einsum('bhqk,bhkd->bhqd', att, v)
        out = out.transpose(0, 2, 1, 3).reshape(B, Nq, HEADS * D_K)
        out = out @ Wo.T + bo
        out = queries + out
        mean = jnp.mean(out, axis=-1, keepdims=True)
        var = jnp.var(out, axis=-1, keepdims=True)
        out = (out - mean) / jnp.sqrt(var + 1e-05) * gamma + beta
        return out
    x = _L0_xattn_ref(x, ctx_1024, ctx_1024, L0_xattn_Wq, L0_xattn_bq, L0_xattn_Wk, L0_xattn_bk, L0_xattn_Wv, L0_xattn_bv, L0_xattn_Wo, L0_xattn_bo, L0_xattn_gamma, L0_xattn_beta)
    return x

_drawn_inputs = setup_inputs


def setup_inputs(seed=0):
    import zlib

    import numpy as np

    out = dict(_drawn_inputs(seed))
    spreads = {'L0_xattn_bq': (0.0, 0.422),
     'L0_xattn_bk': (0.0, 0.8),
     'L0_xattn_bv': (0.0, 0.1),
     'L0_xattn_bo': (0.0, 0.1),
     'L0_xattn_gamma': (1.0, 0.2),
     'L0_xattn_beta': (0.0, 0.1)}
    factors = {}
    for name, (base, spread) in spreads.items():
        noise = np.random.default_rng([zlib.crc32(name.encode()), seed]).standard_normal(out[name].shape)
        drawn = base * np.exp(spread * noise) if base else spread * noise
        out[name] = jnp.asarray(drawn.astype(out[name].dtype))
    for name, factor in factors.items():
        out[name] = (out[name] * factor).astype(out[name].dtype)
    return out
```

```python
from contextlib import ExitStack, nullcontext

import concourse.bass as bass
from concourse import mybir

F32 = mybir.dt.float32
F16 = mybir.dt.float16
ALU = mybir.AluOpType
ACT = mybir.ActivationFunctionType
AX = mybir.AxisListType

WSCALE = 16.0
DMA = 16


def build(nc, x, ctx_tokens, Wq, bq, Wk, bk, Wv, bv, Wo, bo, gamma, beta, out):
    B, NQ, D = x.shape
    NK = ctx_tokens.shape[1]
    HEADS = 16
    DK = D // HEADS
    P = 128
    DT = D // P
    QP = NQ // 2
    KT = 6
    KP = NK // KT
    KH = NK // 2
    HG = P // DK
    UNITS = HEADS // HG
    UNIT = 2 * HG
    STEPS = UNIT * UNITS
    LAST = B - 1
    assert QP * 2 == NQ and KP * KT == NK and UNITS % 2 == 0 and 3 * DK <= P
    SCORE_SCALE = 1.0 / (WSCALE * WSCALE * float(DK) ** 0.5)
    SPLIT_ROWS = ((0, 0), (1, 0), (0, 1))
    STACK_DMAS = 2 * HG * len(SPLIT_ROWS)

    PROJECT = {0: ("ctxT", 0), 1: ("ctxT", 1), 2: ("ctxT", 2), 3: ("ctxT", 3), 4: ("V", 0), 5: ("ctxT", 4),
               6: ("V", 1), 7: ("ctxT", 5), 8: ("V", 2), 9: ("xT", 0), 10: ("V", 3), 11: ("xT", 1),
               12: ("V", 4), 14: ("V", 5)}
    for g in range(UNITS):
        PROJECT.update({16 + 3 * g: ("K", g, 0), 17 + 3 * g: ("K", g, 1), 18 + 3 * g: ("Q", g)})
    OUTPUT = {13: ("O", 0), 15: ("O", 1)}
    SPLIT_KINDS = ("ctxT", "xT", "K", "Q", "W")
    prologue = ([("ctxT", i) for i in range(KT)] + [("W", "k", k) for k in range(DT)] + [("xT", 0), ("xT", 1)]
                + [("W", "q", k) for k in range(DT)])
    for g in range(UNITS):
        prologue += [("K", g, 0), ("K", g, 1), ("Q", g)]
    prologue += [("W", "v", k) for k in range(DT)] + [("V", i) for i in range(KT)]
    prologue += [("W", "o", k) for k in range(DT)]
    PRO = len(prologue)
    PRO_SPLITS = sum(t[0] in SPLIT_KINDS for t in prologue)
    PRO_BANKS = 4

    def has_a(b):
        return not (isinstance(b, int) and b == LAST)

    def has_o(b):
        return not (isinstance(b, int) and b == 0)

    def iteration_tasks(b):
        every = dict(PROJECT if has_a(b) else {})
        every.update(OUTPUT if has_o(b) else {})
        found, splits = {}, 0
        for place, s in enumerate(sorted(every)):
            found[s] = (every[s], place, splits)
            splits += every[s][0] in SPLIT_KINDS
        return found

    def tasks_before(b):
        if isinstance(b, int) and b == 0:
            return PRO
        return PRO - len(OUTPUT) + (len(PROJECT) + len(OUTPUT)) * b

    A_SPLITS = sum(t[0] in SPLIT_KINDS for t in PROJECT.values())

    def splits_before(b):
        return PRO_SPLITS + A_SPLITS * b

    LAST_CTX = max(s for s, t in PROJECT.items() if t[0] == "ctxT")
    LAST_X = max(s for s, t in PROJECT.items() if t[0] == "xT")

    with ExitStack() as stack:
        def sb(name, shape, dt=F32):
            return stack.enter_context(nc.sbuf_tensor(name, shape, dt))

        def psum(name, shape):
            return stack.enter_context(nc.psum_tensor(name, shape, F32))

        def sem(name):
            return stack.enter_context(nc.semaphore(name))

        ps_scores = psum("ps_scores", [P, 4, 512])
        ps_probsT = psum("ps_probsT", [P, 2, 512])
        ps_attn = psum("ps_attn", [P, 512])
        ps_task = psum("ps_task", [P, 512])
        SPREAD = 256

        wT = {w: sb(f"w{w}T", [P, 2, DT, D], F16) for w in "qkvo"}
        ctx_in = sb("ctx_in", [P, KT, D])
        x_in = sb("x_in", [P, 2, D])
        ctxT = sb("ctxT", [P, 2, DT, NK], F16)
        xT = sb("xT", [P, 2, DT, NQ], F16)
        k_parts = sb("k_parts", [P, 2, 2, NK], F16)
        q_parts = sb("q_parts", [P, 2, 2, NQ], F16)
        k_stack = sb("k_stack", [3 * DK, UNITS, HG, NK], F16)
        q_stack = sb("q_stack", [3 * DK, UNITS, HG, NQ], F16)
        v_next = sb("v_next", [P, KT, D])
        v_now = sb("v_now", [P, KT, D])
        probs = sb("probs", [P, 4, NK])
        probsT = sb("probsT", [P, 2, HG, KT, NQ])
        w_in = probsT[:].rearrange("p u h k q -> p (u h k q)")[:, 0:4 * DT * D].rearrange(
            "p (w t d) -> p w t d", w=4, t=DT)
        top = sb("top", [P, 4])
        shift = sb("shift", [P, 4])
        neg_scale = sb("neg_scale", [P, 1])
        sums = sb("sums", [P, 2, UNIT])
        recip = sb("recip", [P, UNIT])
        recip_wide = sb("recip_wide", [P, 2, HG, DK])
        ones = sb("ones", [P, HG, DK])
        spread = sb("spread", [P, NQ])
        attn = sb("attn", [P, NQ])
        attn_parts = sb("attn_parts", [P, 2, UNITS, NQ], F16)
        resid = sb("resid", [P, 2, D])
        y = sb("y", [P, 2, D])
        stats = sb("stats", [P, 2, 6])
        mean_var = sb("mean_var", [P, 2, 2])
        var_eps = sb("var_eps", [P, 2])
        rstd = sb("rstd", [P, 2])
        eps = sb("eps", [P, 1])
        minus_half = sb("minus_half", [P, 1])
        bias = {w: sb(f"b{w}_in", [P, DT]) for w in "qkv"}
        bias16 = {w: sb(f"b{w}16", [P, DT]) for w in "qkv"}
        rows = {n: sb(f"{n}_row", [P, D]) for n in ("gamma", "beta", "bo")}
        ident = sb("ident", [P, P])

        ctx_loaded, x_loaded = sem("ctx_loaded"), sem("x_loaded")
        w_loaded = {w: sem(f"w{w}_loaded") for w in "qkvo"}
        bias_loaded, rows_loaded = sem("bias_loaded"), sem("rows_loaded")
        resid_loaded = sem("resid_loaded")
        stacked = [sem(f"stacked{g}") for g in range(UNITS)]
        v_moved = [sem(f"v_moved{k}") for k in range(KT)]
        stored = sem("stored")
        scores_ready, probsT_lo_ready, probsT_hi_ready = sem("scores_ready"), sem("probsT_lo_ready"), sem("probsT_hi_ready")
        task_ready, attn_ready, spread_ready = sem("task_ready"), sem("attn_ready"), sem("spread_ready")
        probs_ready, probsT_lo_saved, high_saved = sem("probs_ready"), sem("probsT_lo_saved"), sem("high_saved")
        spread_saved, attn_high_saved = sem("spread_saved"), sem("attn_high_saved")
        top_ready, probsT_hi_saved, task_saved = sem("top_ready"), sem("probsT_hi_saved"), sem("task_saved")
        recip_ready, attn_scaled, attn_low_saved = sem("recip_ready"), sem("attn_scaled"), sem("attn_low_saved")
        stats_ready, mean_ready, centered, bias_ready = sem("stats_ready"), sem("mean_ready"), sem("centered"), sem("bias_ready")
        const_ready, ident_zero, ident_ready, shift_ready = sem("const_ready"), sem("ident_zero"), sem("ident_ready"), sem("shift_ready")
        wide_ready, resid_ready, var_eps_ready, rstd_ready = sem("wide_ready"), sem("resid_ready"), sem("var_eps_ready"), sem("rstd_ready")
        y_scaled, y_ready = sem("y_scaled"), sem("y_ready")

        def need(eng, s, value):
            if not isinstance(value, int) or value > 0:
                eng.wait_ge(s, value)

        def dram(t, b):
            return t[b] if isinstance(b, int) else t[bass.ds(b, 1)].rearrange("a t d -> (a t) d")

        def batches(eng, iteration):
            iteration(0)
            with eng.Fori(1, LAST) as b:
                iteration(b)
            iteration(LAST)

        def unit_before(b, g, back):
            u = UNITS * b + g - back
            return None if isinstance(u, int) and u < 0 else u

        def split_views(t, bank, part):
            kind = t[0]
            if kind == "ctxT":
                i = t[1]
                return ctxT[:, part, :, KP * i:KP * i + KP], bank[:, 0:DT * KP].rearrange("p (k t) -> p k t", k=DT), None
            if kind == "xT":
                i = t[1]
                return xT[:, part, :, QP * i:QP * i + QP], bank[:, 0:DT * QP].rearrange("p (k t) -> p k t", k=DT), None
            if kind == "W":
                return wT[t[1]][:, part, t[2], :], bank[:, :], None
            g = t[1]
            if kind == "K":
                return k_parts[:, g % 2, part, KH * t[2]:KH * t[2] + KH], bank[:, 0:KH], bias16["k"][:, g:g + 1]
            return q_parts[:, g % 2, part, :], bank[:, 0:NQ], bias16["q"][:, g:g + 1]

        def wait_parts_free(eng, g, batch):
            if g >= 2:
                eng.wait_ge(stacked[g - 2], DMA * STACK_DMAS * (batch + 1))
            else:
                need(eng, stacked[g + 2], DMA * STACK_DMAS * batch)

        block = stack.enter_context(nc.Block())

        @block.sync
        def _(sp):
            def load_ctx(b):
                sp.dma_start(ctx_in[0:KP], dram(ctx_tokens, b).rearrange("(k p) d -> p k d", p=KP)).then_inc(ctx_loaded, DMA)

            def load_x(b):
                sp.dma_start(x_in[0:QP], dram(x, b).rearrange("(q p) d -> p q d", p=QP)).then_inc(x_loaded, DMA)

            def load_resid(b):
                sp.dma_start(resid[0:QP], dram(x, b).rearrange("(q p) d -> p q d", p=QP)).then_inc(resid_loaded, DMA)

            def stack_unit(g):
                for h in range(HG):
                    rows_of_h = slice(DK * h, DK * h + DK)
                    for r, (q_part, k_part) in enumerate(SPLIT_ROWS):
                        to = slice(DK * r, DK * r + DK)
                        sp.dma_start(k_stack[to, g, h, :], k_parts[rows_of_h, g % 2, k_part, :]).then_inc(stacked[g], DMA)
                        sp.dma_start(q_stack[to, g, h, :], q_parts[rows_of_h, g % 2, q_part, :]).then_inc(stacked[g], DMA)

            def move_v(k):
                sp.dma_start(v_now[0:KP, k], v_next[0:KP, k]).then_inc(v_moved[k], DMA)

            def store(b, q):
                sp.dma_start(dram(out, b).rearrange("(q p) d -> p q d", p=QP)[:, q], y[0:QP, q]).then_inc(stored, DMA)

            load_ctx(0)
            for i, (w, W) in enumerate((("k", Wk), ("q", Wq), ("v", Wv), ("o", Wo))):
                sp.dma_start(w_in[:, "qkvo".index(w)], W.rearrange("(t p) d -> p t d", p=P)).then_inc(w_loaded[w], DMA)
                if i == 0:
                    load_x(0)
                    for name, v in (("k", bk), ("q", bq), ("v", bv)):
                        sp.dma_start(bias[name][:], v.rearrange("(t p) -> p t", p=P), allow_slow_non_contiguous=True).then_inc(bias_loaded, DMA)
            for name, v in (("gamma", gamma), ("beta", beta), ("bo", bo)):
                sp.dma_start(rows[name][0:QP], v.partition_broadcast(QP)).then_inc(rows_loaded, DMA)
            sp.wait_ge(task_ready, KT)
            load_ctx(1)
            sp.wait_ge(task_ready, prologue.index(("xT", 1)) + 1)
            load_x(1)
            for g in range(UNITS):
                sp.wait_ge(task_saved, prologue.index(("Q", g)) + 1)
                stack_unit(g)
            for k in range(KT):
                sp.wait_ge(task_saved, prologue.index(("V", k)) + 1)
                move_v(k)
            load_resid(0)

            def iteration(b):
                tasks = iteration_tasks(b)
                before = tasks_before(b)
                if has_o(b):
                    sp.wait_ge(task_saved, before)
                    for k in range(KT):
                        sp.wait_ge(attn_ready, KT * (UNITS * b - 1) + k + 1)
                        move_v(k)
                if has_a(b) and not (isinstance(b, int) and b == LAST - 1):
                    sp.wait_ge(task_ready, before + tasks[LAST_CTX][1] + 1)
                    load_ctx(b + 2)
                    sp.wait_ge(task_ready, before + tasks[LAST_X][1] + 1)
                    load_x(b + 2)
                if has_o(b):
                    for q in range(2):
                        sp.wait_ge(y_ready, 2 * (b - 1) + q + 1)
                        store(b - 1, q)
                    sp.wait_ge(task_saved, before + tasks[15][1] + 1)
                    load_resid(b)
                if has_a(b):
                    for g in range(UNITS):
                        if UNIT * (g + 1) <= 18 + 3 * g:
                            sp.wait_ge(task_saved, before + tasks[18 + 3 * g][1] + 1)
                        else:
                            sp.wait_ge(scores_ready, STEPS * (b + 1))
                        stack_unit(g)

            iteration(0)
            with sp.Fori(1, LAST - 1) as b:
                iteration(b)
            iteration(LAST - 1)
            iteration(LAST)
            for q in range(2):
                sp.wait_ge(y_ready, 2 * LAST + q + 1)
                store(LAST, q)
            sp.wait_ge(stored, DMA * 2 * B)

        @block.tensor
        def _(pe):
            def task(t, n, bank, batch):
                kind = t[0]
                if kind == "ctxT":
                    pe.wait_ge(ctx_loaded, DMA * (batch + 1))
                    for k in range(DT):
                        last = nc.tensor.transpose(bank[:, KP * k:KP * k + KP], ctx_in[0:KP, t[1], P * k:P * k + P], ident[0:KP, 0:KP])
                elif kind == "xT":
                    pe.wait_ge(x_loaded, DMA * (batch + 1))
                    for k in range(DT):
                        last = nc.tensor.transpose(bank[:, QP * k:QP * k + QP], x_in[0:QP, t[1], P * k:P * k + P], ident[0:QP, 0:QP])
                elif kind == "W":
                    pe.wait_ge(w_loaded[t[1]], DMA)
                    for f in range(DT):
                        last = nc.tensor.transpose(bank[:, P * f:P * f + P], w_in[:, "qkvo".index(t[1]), f, P * t[2]:P * t[2] + P], ident[:])
                else:
                    first, n_mm = True, 3 * DT
                    for k in range(DT):
                        for a, c in ((0, 0), (0, 1), (1, 0)):
                            if kind == "K":
                                g, half = t[1], t[2]
                                dst, lhsT, rhs = bank[:, 0:KH], wT["k"][:, a, k, P * g:P * g + P], ctxT[:, c, k, KH * half:KH * half + KH]
                            elif kind == "Q":
                                g = t[1]
                                dst, lhsT, rhs = bank[:, 0:NQ], wT["q"][:, a, k, P * g:P * g + P], xT[:, c, k, :]
                            elif kind == "V":
                                i = t[1]
                                dst, lhsT, rhs = bank[0:KP, :], ctxT[:, a, k, KP * i:KP * i + KP], wT["v"][:, c, k, :]
                            else:
                                q = t[1]
                                dst, lhsT, rhs = bank[0:QP, :], attn_parts[:, a, k, QP * q:QP * q + QP], wT["o"][:, c, k, :]
                            n_mm -= 1
                            last = nc.tensor.matmul(dst, lhsT, rhs, start=first, stop=(n_mm == 0))
                            first = False
                last.then_inc(task_ready, 1)

            def scores(s, first_of_unit, batch, q_of_step=None):
                g, h, q = s // UNIT, s % UNIT // 2, s % 2
                if first_of_unit:
                    pe.wait_ge(stacked[g], DMA * STACK_DMAS * (batch + 1))
                for c in range(2):
                    last = nc.tensor.matmul(ps_scores[0:QP, 2 * (s % 2) + c, 0:KH], q_stack[:, g, h, QP * q:QP * q + QP],
                                            k_stack[:, g, h, KH * c:KH * c + KH], start=True, stop=True)
                last.then_inc(scores_ready, 1)

            def transpose_probs(s, T):
                need(pe, probs_ready, T + 1)
                need(pe, probsT_lo_saved, T)
                for half, ready in ((0, probsT_lo_ready), (1, probsT_hi_ready)):
                    if half:
                        need(pe, probsT_hi_saved, T)
                    for i in range(3):
                        k = 3 * half + i
                        last = nc.tensor.transpose(ps_probsT[0:KP, half, QP * i:QP * i + QP],
                                                   probs[0:QP, s % 4, KP * k:KP * k + KP], ident[0:QP, 0:QP])
                    last.then_inc(ready, 1)

            def attend(u, g, k, batch):
                if k == 0:
                    need(pe, probsT_lo_saved, UNIT * (u + 1))
                    need(pe, attn_scaled, u)
                if k == 3:
                    need(pe, probsT_hi_saved, UNIT * (u + 1))
                if g == 0:
                    pe.wait_ge(v_moved[k], DMA * (batch + 1))
                for h in range(HG):
                    c = DK * h
                    last = nc.tensor.matmul(ps_attn[c:c + DK, 0:NQ], v_now[0:KP, k, P * g + c:P * g + c + DK],
                                            probsT[0:KP, g % 2, h, k, :], start=(k == 0), stop=(k == KT - 1),
                                            tile_position=(0, c))
                last.then_inc(attn_ready, 1)

            def spread_recip(u):
                need(pe, wide_ready, u + 1)
                for q in range(2):
                    last = nc.tensor.matmul(ps_attn[:, SPREAD + QP * q:SPREAD + QP * q + QP],
                                            recip_wide[0:QP, q].rearrange("p h d -> p (h d)"), ident[0:QP, 0:QP],
                                            start=True, stop=True)
                last.then_inc(spread_ready, 1)

            pe.wait_ge(ident_ready, 1)
            for n, t in enumerate(prologue):
                if n >= PRO_BANKS:
                    pe.wait_ge(task_saved, n - PRO_BANKS + 1)
                if t[0] == "K" and t[1:] == (0, 0):
                    pe.wait_ge(task_saved, prologue.index(("W", "k", DT - 1)) + 1)
                if t == ("Q", 0):
                    pe.wait_ge(task_saved, prologue.index(("W", "q", DT - 1)) + 1)
                if t == ("V", 0):
                    pe.wait_ge(task_saved, prologue.index(("W", "v", DT - 1)) + 1)
                task(t, n, ps_scores[:, n % PRO_BANKS], 0)
            pe.wait_ge(task_saved, PRO)
            scores(0, True, 0)

            def iteration(b):
                tasks = iteration_tasks(b)
                before = tasks_before(b)
                for s in range(STEPS):
                    T = STEPS * b + s
                    g = s // UNIT
                    if not (isinstance(b, int) and b == LAST and s == STEPS - 1):
                        need(pe, probs_ready, T)
                        scores((s + 1) % STEPS, (s + 1) % UNIT == 0, b if s < STEPS - 1 else b + 1)
                    if not (isinstance(b, int) and b == 0 and s == 0):
                        transpose_probs((s - 1) % STEPS, T - 1)
                    u = unit_before(b, g, 1)
                    if u is not None:
                        if 2 <= s % UNIT:
                            attend(u, (g - 1) % UNITS, s % UNIT - 2, b if g else b - 1)
                        if s % UNIT == UNIT - 1:
                            spread_recip(u)
                    if s in tasks:
                        t, place, _ = tasks[s]
                        pe.wait_ge(task_saved, before + place)
                        if t == ("O", 0):
                            pe.wait_ge(attn_low_saved, UNITS * b)
                        task(t, before + place, ps_task, b + 1)

            batches(pe, iteration)
            T, u = STEPS * B, UNITS * B - 1
            transpose_probs(STEPS - 1, T - 1)
            for k in range(KT):
                attend(u, UNITS - 1, k, LAST)
            spread_recip(u)
            n = tasks_before(LAST) + len(OUTPUT)
            pe.wait_ge(attn_low_saved, u + 1)
            for q in range(2):
                pe.wait_ge(task_saved, n + q)
                task(("O", q), n + q, ps_task, B)

        @block.scalar
        def _(act):
            def high_part(t, n, bank, batch):
                if t[0] not in SPLIT_KINDS:
                    return
                if t[0] in "KQ":
                    wait_parts_free(act, t[1], batch)
                act.wait_ge(task_ready, n + 1)
                dst, src, b16 = split_views(t, bank, 0)
                if b16 is not None:
                    nc.scalar.activation(dst, src, ACT.Identity, bias=b16).then_inc(high_saved, 1)
                else:
                    nc.scalar.activation(dst, src, ACT.Copy, scale=WSCALE if t[0] == "W" else 1.0).then_inc(high_saved, 1)

            def exp(s, T):
                g = s // UNIT
                act.wait_ge(shift_ready, T + 1)
                if isinstance(T, int) and T < 4:
                    pass
                else:
                    act.wait_ge(probsT_hi_ready, T - 3)
                nc.scalar.activation(probs[0:QP, s % 4, :].rearrange("p (c k) -> p c k", c=2),
                                     ps_scores[0:QP, 2 * (s % 2):2 * (s % 2) + 2, 0:KH], ACT.Exp,
                                     bias=shift[0:QP, s % 4:s % 4 + 1], scale=SCORE_SCALE,
                                     accum_out=sums[0:QP, g % 2, s % UNIT:s % UNIT + 1]).then_inc(probs_ready, 1)

            def save_probsT(s, T, wait_unit):
                g, h, q = s // UNIT, s % UNIT // 2, s % 2
                act.wait_ge(probsT_lo_ready, T + 1)
                if wait_unit is not None:
                    need(act, attn_ready, wait_unit)
                nc.scalar.activation(probsT[0:KP, g % 2, h, 0:3, QP * q:QP * q + QP],
                                     ps_probsT[0:KP, 0, 0:3 * QP].rearrange("p (k q) -> p k q", k=3),
                                     ACT.Copy).then_inc(probsT_lo_saved, 1)

            def save_spread(u):
                act.wait_ge(spread_ready, u + 1)
                need(act, attn_scaled, u)
                nc.scalar.activation(spread[:], ps_attn[:, SPREAD:SPREAD + NQ], ACT.Copy).then_inc(spread_saved, 1)

            def attn_high(u, g, task_n):
                act.wait_ge(attn_scaled, u + 1)
                if task_n is not None:
                    act.wait_ge(task_ready, task_n)
                nc.scalar.activation(attn_parts[:, 0, g, :], attn[:], ACT.Identity,
                                     bias=bias16["v"][:, g:g + 1]).then_inc(attn_high_saved, 1)

            act.wait_ge(bias_ready, 3)
            for n, t in enumerate(prologue):
                high_part(t, n, ps_scores[:, n % PRO_BANKS], 0)
            exp(0, 0)

            def iteration(b):
                tasks = iteration_tasks(b)
                before = tasks_before(b)
                for s in range(STEPS):
                    T = STEPS * b + s
                    g = s // UNIT
                    if s - 1 in tasks:
                        t, place, _ = tasks[s - 1]
                        high_part(t, before + place, ps_task, b + 1)
                    if not (isinstance(b, int) and b == 0 and s == 0):
                        u1 = unit_before(b, g, 1)
                        save_probsT((s - 1) % STEPS, T - 1, KT * u1 if s % UNIT == 1 and u1 is not None else None)
                    if s % UNIT == 0 and unit_before(b, g, 2) is not None:
                        save_spread(unit_before(b, g, 2))
                    if not (isinstance(b, int) and b == LAST and s == STEPS - 1):
                        if (s + 1) % UNIT == 0 and unit_before(b, g, 1) is not None:
                            act.wait_ge(recip_ready, UNITS * b + g)
                        exp((s + 1) % STEPS, T + 1)
                    if s % UNIT == 1 and unit_before(b, g, 2) is not None:
                        after_o = before + tasks[15][1] + 1 if (g == 2 and has_o(b)) else None
                        attn_high(unit_before(b, g, 2), (g - 2) % UNITS, after_o)

            batches(act, iteration)
            T, u = STEPS * B, UNITS * B - 1
            save_probsT(STEPS - 1, T - 1, None)
            save_spread(u - 1)
            attn_high(u - 1, UNITS - 2, None)
            save_spread(u)
            attn_high(u, UNITS - 1, None)

        @block.vector
        def _(dve):
            def save_task(t, n, splits, bank, batch):
                kind = t[0]
                if kind in SPLIT_KINDS:
                    dst, src, b16 = split_views(t, bank, 1)
                    high = split_views(t, bank, 0)[0]
                    if kind in "KQ":
                        wait_parts_free(dve, t[1], batch)
                    dve.wait_ge(high_saved, splits + 1)
                    if kind == "W":
                        nc.vector.scalar_tensor_tensor(dst, src, WSCALE, high, ALU.mult, ALU.subtract).then_inc(task_saved, 1)
                    elif b16 is not None:
                        nc.vector.scalar_tensor_tensor(dst, src, b16, high, ALU.add, ALU.subtract).then_inc(task_saved, 1)
                    else:
                        nc.vector.tensor_tensor(dst, src, high, ALU.subtract).then_inc(task_saved, 1)
                elif kind == "V":
                    dve.wait_ge(task_ready, n + 1)
                    need(dve, v_moved[t[1]], DMA * batch)
                    nc.vector.tensor_copy(v_next[0:KP, t[1]], bank[0:KP, :]).then_inc(task_saved, 1)
                else:
                    q = t[1]
                    dve.wait_ge(task_ready, n + 1)
                    need(dve, stored, 2 * DMA * batch)
                    if q == 0:
                        dve.wait_ge(resid_ready, 2 * (batch + 1))
                    nc.vector.scalar_tensor_tensor(y[0:QP, q], bank[0:QP, :], 1.0 / (WSCALE * WSCALE), resid[0:QP, q],
                                                   ALU.mult, ALU.add).then_inc(task_saved, 1)
                    dve.wait_ge(task_saved, n + 1)
                    nc.vector.bn_stats(stats[0:QP, q], y[0:QP, q]).then_inc(stats_ready, 1)

            def mean_of(q, batch):
                if isinstance(batch, int):
                    dve.wait_ge(stats_ready, 2 * batch + q + 1)
                nc.vector.bn_aggr(mean_var[0:QP, q], stats[0:QP, q]).then_inc(mean_ready, 1)

            def center(q, batch):
                dve.wait_ge(rstd_ready, 2 * batch + q + 1)
                nc.vector.tensor_scalar(y[0:QP, q], y[0:QP, q], mean_var[0:QP, q, 0:1], rstd[0:QP, q:q + 1],
                                        ALU.subtract, ALU.mult).then_inc(centered, 1)

            def row_max(s, T, stats_of=None):
                if stats_of is not None:
                    dve.wait_ge(stats_ready, stats_of)
                dve.wait_ge(scores_ready, T + 1)
                nc.vector.tensor_reduce(top[0:QP, s % 4:s % 4 + 1], ps_scores[0:QP, 2 * (s % 2):2 * (s % 2) + 2, 0:KH],
                                        AX.XY, ALU.max).then_inc(top_ready, 1)

            def save_probsT(s, T, wait_unit):
                g, h, q = s // UNIT, s % UNIT // 2, s % 2
                dve.wait_ge(probsT_hi_ready, T + 1)
                if wait_unit is not None:
                    need(dve, attn_ready, wait_unit)
                nc.vector.tensor_copy(probsT[0:KP, g % 2, h, 3:6, QP * q:QP * q + QP],
                                      ps_probsT[0:KP, 1, 0:3 * QP].rearrange("p (k q) -> p k q", k=3)).then_inc(probsT_hi_saved, 1)

            def invert_sums(u, g):
                dve.wait_ge(probs_ready, UNIT * (u + 1))
                need(dve, wide_ready, u)
                nc.vector.reciprocal(recip[0:QP], sums[0:QP, g % 2]).then_inc(recip_ready, 1)

            def scale_attn(u):
                dve.wait_ge(spread_saved, u + 1)
                need(dve, attn_high_saved, u)
                need(dve, attn_low_saved, u)
                nc.vector.tensor_tensor(attn[:], ps_attn[:, 0:NQ], spread[:], ALU.mult).then_inc(attn_scaled, 1)

            def attn_low(u, g):
                dve.wait_ge(attn_high_saved, u + 1)
                nc.vector.scalar_tensor_tensor(attn_parts[:, 1, g, :], attn[:], bias16["v"][:, g:g + 1],
                                               attn_parts[:, 0, g, :], ALU.add, ALU.subtract).then_inc(attn_low_saved, 1)

            dve.wait_ge(bias_loaded, 3 * DMA)
            for w in "qkv":
                nc.vector.tensor_scalar(bias16[w][:], bias[w][:], WSCALE, None, ALU.mult).then_inc(bias_ready, 1)
            dve.wait_ge(bias_ready, 3)
            splits = 0
            for n, t in enumerate(prologue):
                save_task(t, n, splits, ps_scores[:, n % PRO_BANKS], 0)
                splits += t[0] in SPLIT_KINDS
            row_max(0, 0)

            def iteration(b):
                tasks = iteration_tasks(b)
                before = tasks_before(b)
                for s in range(STEPS):
                    T = STEPS * b + s
                    g = s // UNIT
                    if s - 1 in tasks:
                        t, place, splits = tasks[s - 1]
                        save_task(t, before + place, splits_before(b) + splits, ps_task, b - 1 if t[0] == "O" else b + 1)
                    if not (isinstance(b, int) and b == LAST and s == STEPS - 1):
                        aggregate = s - 14 if has_o(b) and s in (14, 16) else None
                        row_max((s + 1) % STEPS, T + 1, None if aggregate is None else 2 * (b - 1) + aggregate // 2 + 1)
                        if aggregate is not None:
                            mean_of(aggregate // 2, b - 1)
                    if not (isinstance(b, int) and b == 0 and s == 0):
                        u1 = unit_before(b, g, 1)
                        save_probsT((s - 1) % STEPS, T - 1, KT * u1 if s % UNIT == 1 and u1 is not None else None)
                    if s % UNIT == 0 and unit_before(b, g, 2) is not None:
                        scale_attn(unit_before(b, g, 2))
                    if s % UNIT == 2 and unit_before(b, g, 2) is not None:
                        attn_low(unit_before(b, g, 2), (g - 2) % UNITS)
                    if s % UNIT == 1 and unit_before(b, g, 1) is not None:
                        invert_sums(unit_before(b, g, 1), (g - 1) % UNITS)
                    if has_o(b):
                        for q in range(2):
                            if s == 16 + 2 * q:
                                center(q, b - 1)

            batches(dve, iteration)
            T, u = STEPS * B, UNITS * B - 1
            save_probsT(STEPS - 1, T - 1, None)
            invert_sums(u, UNITS - 1)
            scale_attn(u - 1)
            attn_low(u - 1, UNITS - 2)
            scale_attn(u)
            attn_low(u, UNITS - 1)
            n = tasks_before(LAST) + len(OUTPUT)
            for q in range(2):
                save_task(("O", q), n + q, None, ps_task, LAST)
                mean_of(q, LAST)
            for q in range(2):
                center(q, LAST)

        @block.gpsimd
        def _(pool):
            nc.gpsimd.memset(ident[:], 0.0).then_inc(ident_zero, 1)
            pool.wait_ge(ident_zero, 1)
            nc.gpsimd.affine_select(out=ident[:], in_=ident[:], compare_op=ALU.not_equal, fill=1.0, base=0,
                                    pattern=[[-1, P]], channel_multiplier=1).then_inc(ident_ready, 1)
            nc.gpsimd.memset(neg_scale[:], -SCORE_SCALE).then_inc(const_ready, 1)
            nc.gpsimd.memset(ones[:], 1.0).then_inc(const_ready, 1)
            nc.gpsimd.memset(eps[:], 1e-5).then_inc(const_ready, 1)
            nc.gpsimd.memset(minus_half[:], -0.5).then_inc(const_ready, 1)
            pool.wait_ge(const_ready, 4)

            def row_shift(s, T):
                pool.wait_ge(top_ready, T + 1)
                nc.gpsimd.tensor_tensor(shift[0:QP, s % 4:s % 4 + 1], top[0:QP, s % 4:s % 4 + 1], neg_scale[0:QP],
                                        ALU.mult).then_inc(shift_ready, 1)

            def widen(u):
                pool.wait_ge(recip_ready, u + 1)
                need(pool, spread_ready, u)
                for q in range(2):
                    r = recip[0:QP].rearrange("p (h q) -> p h q", q=2)[:, :, q:q + 1]
                    last = nc.gpsimd.tensor_tensor(recip_wide[0:QP, q], r.broadcast_to([QP, HG, DK]), ones[0:QP], ALU.mult)
                last.then_inc(wide_ready, 1)

            def add_bo(q, batch):
                if q == 0:
                    pool.wait_ge(resid_loaded, DMA * (batch + 1))
                nc.gpsimd.tensor_tensor(resid[0:QP, q], resid[0:QP, q], rows["bo"][0:QP], ALU.add).then_inc(resid_ready, 1)

            def rstd_of(q, batch):
                pool.wait_ge(mean_ready, 2 * batch + q + 1)
                nc.gpsimd.tensor_tensor(var_eps[0:QP, q:q + 1], mean_var[0:QP, q, 1:2], eps[0:QP], ALU.add).then_inc(var_eps_ready, 1)
                pool.wait_ge(var_eps_ready, 2 * batch + q + 1)
                nc.gpsimd.tensor_tensor(rstd[0:QP, q:q + 1], var_eps[0:QP, q:q + 1], minus_half[0:QP], ALU.pow).then_inc(rstd_ready, 1)

            def times_gamma(q, batch):
                pool.wait_ge(centered, 2 * batch + q + 1)
                nc.gpsimd.tensor_tensor(y[0:QP, q], y[0:QP, q], rows["gamma"][0:QP], ALU.mult).then_inc(y_scaled, 1)

            def plus_beta(q, batch):
                pool.wait_ge(y_scaled, 2 * batch + q + 1)
                nc.gpsimd.tensor_tensor(y[0:QP, q], y[0:QP, q], rows["beta"][0:QP], ALU.add).then_inc(y_ready, 1)

            row_shift(0, 0)
            pool.wait_ge(rows_loaded, 3 * DMA)

            def iteration(b):
                for s in range(STEPS):
                    T = STEPS * b + s
                    g = s // UNIT
                    if not (isinstance(b, int) and b == LAST and s == STEPS - 1):
                        row_shift((s + 1) % STEPS, T + 1)
                    if s % UNIT == 2 and unit_before(b, g, 1) is not None:
                        widen(unit_before(b, g, 1))
                    if has_o(b):
                        for q in range(2):
                            if s == 8 + q:
                                add_bo(q, b - 1)
                            if s == 14 + 2 * q:
                                rstd_of(q, b - 1)
                            if s == 16 + 2 * q:
                                times_gamma(q, b - 1)
                            if s == 17 + 2 * q:
                                plus_beta(q, b - 1)

            batches(pool, iteration)
            widen(UNITS * B - 1)
            for q in range(2):
                add_bo(q, LAST)
            for q in range(2):
                rstd_of(q, LAST)
            for q in range(2):
                times_gamma(q, LAST)
            for q in range(2):
                plus_beta(q, LAST)


_INS = ["x", "ctx_1024", "L0_xattn_Wq", "L0_xattn_bq", "L0_xattn_Wk", "L0_xattn_bk", "L0_xattn_Wv", "L0_xattn_bv",
        "L0_xattn_Wo", "L0_xattn_bo", "L0_xattn_gamma", "L0_xattn_beta"]


def kernel(**inputs):
    import numpy as np
    import concourse.bacc as bacc
    from concourse.bass_utils import run_bass_kernel_spmd

    nc = bacc.Bacc("TRN2", target_bir_lowering=False, num_devices=1)
    arrays, args = {}, []
    for name in _INS:
        a = np.ascontiguousarray(inputs[name])
        arrays[f"in_{name}"] = a
        args.append(nc.dram_tensor(f"in_{name}", a.shape, mybir.dt.from_np(a.dtype), kind="ExternalInput").ap())
    result = nc.dram_tensor("out_y", inputs["x"].shape, F32, kind="ExternalOutput").ap()
    build(nc, *args, result)
    r = run_bass_kernel_spmd(nc, [arrays], core_ids=[0])
    return r.results[0]["out_y"]
```

```python
from contextlib import ExitStack

import concourse.bass as bass
from concourse import mybir

F32 = mybir.dt.float32
F16 = mybir.dt.float16
ALU = mybir.AluOpType
ACT = mybir.ActivationFunctionType
AX = mybir.AxisListType

WSCALE = 16.0
DMA = 16


def build(nc, x, ctx_tokens, Wq, bq, Wk, bk, Wv, bv, Wo, bo, gamma, beta, out):
    B, NQ, D = x.shape
    NK = ctx_tokens.shape[1]
    HEADS = 16
    DK = D // HEADS
    P = 128
    DT = D // P
    QP = NQ // 2
    KT = 6
    KP = NK // KT
    KH = NK // 2
    HG = P // DK
    UNITS = HEADS // HG
    UNIT = 2 * HG
    STEPS = UNIT * UNITS
    LAST = B - 1
    SCORE_SCALE = 1.0 / (WSCALE * WSCALE * float(DK) ** 0.5)
    SPLIT_ROWS = ((0, 0), (1, 0), (0, 1))
    STACK_ROWS = DK * len(SPLIT_ROWS)
    PAIRS = UNITS // 2
    STACK_DMAS = 5 * HG
    PIECES = 3 * HG
    MAX_SCALE = 1024.0
    NU = B * UNITS
    assert QP * 2 == NQ and KP * KT == NK and UNITS % 2 == 0 and STACK_ROWS + HG <= P and KT == 6

    PROJECT = {**{i: ("ctxT", i) for i in range(KT)}, 6: ("xT", 0), 7: ("xT", 1),
               8: ("K", 0, 0), 9: ("K", 0, 1), 10: ("Q", 0), 11: ("K", 1, 0), 12: ("K", 1, 1), 13: ("Q", 1),
               14: ("V", 0), 15: ("K", 2, 0), 16: ("V", 1), 17: ("K", 2, 1), 18: ("Q", 2), 19: ("V", 2),
               21: ("K", 3, 0), 23: ("V", 3), 24: ("K", 3, 1), 26: ("Q", 3), 28: ("V", 4), 30: ("V", 5)}
    O_STEPS = (20, 22)
    OUTPUT = {O_STEPS[q]: ("O", q) for q in range(2)}
    SPLIT_KINDS = ("ctxT", "xT", "K", "Q", "W")
    prologue = ([("ctxT", i) for i in range(KT)] + [("W", "k", k) for k in range(DT)] + [("xT", 0), ("xT", 1)]
                + [("W", "q", k) for k in range(DT)])
    for g in range(UNITS):
        prologue += [("K", g, 0), ("K", g, 1), ("Q", g)]
    prologue += [("W", "v", k) for k in range(DT)] + [("V", i) for i in range(KT)]
    prologue += [("W", "o", k) for k in range(DT)]
    PRO = len(prologue)
    PRO_SPLITS = sum(t[0] in SPLIT_KINDS for t in prologue)
    PRO_BANKS = 4

    def has_a(b):
        return not (isinstance(b, int) and b >= LAST)

    def has_o(b):
        return not (isinstance(b, int) and b == 0)

    def iteration_tasks(b):
        every = dict(PROJECT if has_a(b) else {})
        every.update(OUTPUT if has_o(b) else {})
        found, splits = {}, 0
        for place, s in enumerate(sorted(every)):
            found[s] = (every[s], place, splits)
            splits += every[s][0] in SPLIT_KINDS
        return found

    def tasks_before(b):
        if isinstance(b, int) and b == 0:
            return PRO
        if isinstance(b, int) and b == B:
            return tasks_before(LAST) + len(OUTPUT)
        return PRO - len(OUTPUT) + (len(PROJECT) + len(OUTPUT)) * b

    A_SPLITS = sum(t[0] in SPLIT_KINDS for t in PROJECT.values())

    def splits_before(b):
        return PRO_SPLITS + A_SPLITS * b

    LAST_CTX = max(s for s, t in PROJECT.items() if t[0] == "ctxT")
    LAST_X = max(s for s, t in PROJECT.items() if t[0] == "xT")

    with ExitStack() as stack:
        def sb(name, shape, dt=F32):
            return stack.enter_context(nc.sbuf_tensor(name, shape, dt))

        def psum(name, shape):
            return stack.enter_context(nc.psum_tensor(name, shape, F32))

        def sem(name):
            return stack.enter_context(nc.semaphore(name))

        ps_scores = psum("ps_scores", [P, 4, 512])
        ps_scoresT = psum("ps_scoresT", [P, 2, 512])
        ps_attn = psum("ps_attn", [P, 512])
        ps_task = psum("ps_task", [P, 512])
        SUMS = 256

        wT = {w: sb(f"w{w}T", [P, 2, DT, D], F16) for w in "qkvo"}
        ctx_in = sb("ctx_in", [P, KT, D])
        x_in = sb("x_in", [P, 2, D])
        ctxT = sb("ctxT", [P, 2, DT, NK], F16)
        xT = sb("xT", [P, 2, DT, NQ], F16)
        KQ = NK + NQ
        Kc, Qc = slice(0, NK), slice(NK, KQ)
        parts = sb("parts", [P, UNITS, 2, KQ], F16)
        stacks = sb("stacks", [STACK_ROWS + HG, UNITS, HG, KQ], F16)
        v_next = sb("v_next", [P, KT, D])
        v_now = sb("v_now", [P, KT, D])
        probsT = sb("probsT", [P, 2, HG, KT, NQ])
        w_in = probsT[:].rearrange("p u h k q -> p (u h k q)")[:, 0:4 * DT * D].rearrange(
            "p (w t d) -> p w t d", w=4, t=DT)
        top = sb("top", [P, 2, 2, HG])
        pair_sums = sb("pair_sums", [P, 2, 3, NQ])
        head_sums = sb("head_sums", [P, 2, HG, NQ])
        ones = sb("ones", [P, DK])
        recip = sb("recip", [P, NQ])
        attn = sb("attn", [P, NQ])
        attn_parts = sb("attn_parts", [P, 2, UNITS, NQ], F16)
        resid = sb("resid", [P, 2, D])
        y = sb("y", [P, 2, D])
        stats = sb("stats", [P, 2, 6])
        mean_var = sb("mean_var", [P, 2, 2])
        var_eps = sb("var_eps", [P, 2])
        rstd = sb("rstd", [P, 2])
        eps = sb("eps", [P, 1])
        minus_half = sb("minus_half", [P, 1])
        bias = {w: sb(f"b{w}_in", [P, DT]) for w in "qkv"}
        bias16 = {w: sb(f"b{w}16", [P, DT]) for w in "qkv"}
        rows = {n: sb(f"{n}_row", [P, D]) for n in ("gamma", "beta", "bo")}
        ident = sb("ident", [P, P])

        ctx_loaded, x_loaded = sem("ctx_loaded"), sem("x_loaded")
        w_loaded = {w: sem(f"w{w}_loaded") for w in "qkvo"}
        bias_loaded, rows_loaded = sem("bias_loaded"), sem("rows_loaded")
        resid_loaded = sem("resid_loaded")
        stacked = [sem(f"stacked{pair}") for pair in range(PAIRS)]
        v_moved = [sem(f"v_moved{k}") for k in range(KT)]
        stored = sem("stored")
        scores_ready, maxima_turned, scoresT_ready = sem("scores_ready"), sem("maxima_turned"), sem("scoresT_ready")
        task_ready, attn_ready, sums_ready = sem("task_ready"), sem("attn_ready"), sem("sums_ready")
        maxima_saved, probs_ready = sem("maxima_saved"), sem("probs_ready")
        high_saved, attn_high_saved = sem("high_saved"), sem("attn_high_saved")
        top_ready, head_sums_ready, task_saved = sem("top_ready"), sem("head_sums_ready"), sem("task_saved")
        recip_ready, attn_scaled, attn_low_saved = sem("recip_ready"), sem("attn_scaled"), sem("attn_low_saved")
        stats_ready, mean_ready, centered, bias_ready = sem("stats_ready"), sem("mean_ready"), sem("centered"), sem("bias_ready")
        ones_ready, ident_zero, ident_ready = sem("ones_ready"), sem("ident_zero"), sem("ident_ready")
        pick_zero, pick_ready, pair_sums_ready = sem("pick_zero"), sem("pick_ready"), sem("pair_sums_ready")
        const_ready, resid_ready, var_eps_ready, rstd_ready = sem("const_ready"), sem("resid_ready"), sem("var_eps_ready"), sem("rstd_ready")
        y_scaled, y_ready = sem("y_scaled"), sem("y_ready")

        def need(eng, s, value):
            if not isinstance(value, int) or value > 0:
                eng.wait_ge(s, value)

        def dram(t, b):
            return t[b] if isinstance(b, int) else t[bass.ds(b, 1)].rearrange("a t d -> (a t) d")

        def batches(eng, iteration):
            iteration(0)
            with eng.Fori(1, LAST - 1) as b:
                iteration(b)
            iteration(LAST - 1)
            iteration(LAST)
            iteration(B)

        def unit_before(b, g, back):
            u = UNITS * b + g - back
            return u if not isinstance(u, int) or 0 <= u < NU else None

        def has_step(b, s):
            return not isinstance(b, int) or 0 <= STEPS * b + s < STEPS * B

        def pieces_of(s):
            i = s % UNIT
            return (2 * i - 4, 2 * i - 3) if i >= 2 else ()

        def split_views(t, bank, part):
            kind = t[0]
            if kind == "ctxT":
                i = t[1]
                return ctxT[:, part, :, KP * i:KP * i + KP], bank[:, 0:DT * KP].rearrange("p (k t) -> p k t", k=DT), None
            if kind == "xT":
                i = t[1]
                return xT[:, part, :, QP * i:QP * i + QP], bank[:, 0:DT * QP].rearrange("p (k t) -> p k t", k=DT), None
            if kind == "W":
                return wT[t[1]][:, part, t[2], :], bank[:, :], None
            g = t[1]
            if kind == "K":
                return parts[:, g, part, KH * t[2]:KH * t[2] + KH], bank[:, 0:KH], bias16["k"][:, g:g + 1]
            return parts[:, g, part, Qc], bank[:, 0:NQ], bias16["q"][:, g:g + 1]

        block = stack.enter_context(nc.Block())

        @block.sync
        def _(sp):
            def load_ctx(b):
                sp.dma_start(ctx_in[0:KP], dram(ctx_tokens, b).rearrange("(k p) d -> p k d", p=KP)).then_inc(ctx_loaded, DMA)

            def load_x(b):
                sp.dma_start(x_in[0:QP], dram(x, b).rearrange("(q p) d -> p q d", p=QP)).then_inc(x_loaded, DMA)

            def load_resid(b):
                sp.dma_start(resid[0:QP], dram(x, b).rearrange("(q p) d -> p q d", p=QP)).then_inc(resid_loaded, DMA)

            def stack_pair(pair):
                us = slice(2 * pair, 2 * pair + 2)
                for h in range(HG):
                    rows_of_h = slice(DK * h, DK * h + DK)
                    for r, (q_part, k_part) in enumerate(SPLIT_ROWS):
                        to = slice(DK * r, DK * r + DK)
                        if q_part == k_part:
                            sp.dma_start(stacks[to, us, h, :], parts[rows_of_h, us, k_part, :]).then_inc(stacked[pair], DMA)
                        else:
                            sp.dma_start(stacks[to, us, h, Kc], parts[rows_of_h, us, k_part, Kc]).then_inc(stacked[pair], DMA)
                            sp.dma_start(stacks[to, us, h, Qc], parts[rows_of_h, us, q_part, Qc]).then_inc(stacked[pair], DMA)

            def move_v(k):
                sp.dma_start(v_now[0:KP, k], v_next[0:KP, k]).then_inc(v_moved[k], DMA)

            def store(b, q):
                sp.dma_start(dram(out, b).rearrange("(q p) d -> p q d", p=QP)[:, q], y[0:QP, q]).then_inc(stored, DMA)

            load_ctx(0)
            for i, (w, W) in enumerate((("k", Wk), ("q", Wq), ("v", Wv), ("o", Wo))):
                sp.dma_start(w_in[:, "qkvo".index(w)], W.rearrange("(t p) d -> p t d", p=P)).then_inc(w_loaded[w], DMA)
                if i == 0:
                    load_x(0)
                    for name, v in (("k", bk), ("q", bq), ("v", bv)):
                        sp.dma_start(bias[name][:], v.rearrange("(t p) -> p t", p=P), allow_slow_non_contiguous=True).then_inc(bias_loaded, DMA)
            for name, v in (("gamma", gamma), ("beta", beta), ("bo", bo)):
                sp.dma_start(rows[name][0:QP], v.partition_broadcast(QP)).then_inc(rows_loaded, DMA)
            sp.wait_ge(task_ready, KT)
            load_ctx(1)
            sp.wait_ge(task_ready, prologue.index(("xT", 1)) + 1)
            load_x(1)
            sp.wait_ge(task_saved, prologue.index(("Q", 1)) + 1)
            stack_pair(0)
            for k in range(KT):
                sp.wait_ge(task_saved, prologue.index(("V", k)) + 1)
                move_v(k)
            load_resid(0)

            def iteration(b):
                tasks = iteration_tasks(b)
                before = tasks_before(b)
                if has_step(b, 0):
                    if isinstance(b, int):
                        sp.wait_ge(task_saved, before)
                    if has_o(b):
                        sp.wait_ge(scoresT_ready, PIECES * UNITS * b)
                    stack_pair(1)
                if has_a(b) and not (isinstance(b, int) and b == LAST - 1):
                    sp.wait_ge(task_ready, before + tasks[LAST_CTX][1] + 1)
                    load_ctx(b + 2)
                    sp.wait_ge(task_ready, before + tasks[LAST_X][1] + 1)
                    load_x(b + 2)
                if has_o(b) and has_step(b, 0):
                    for k in range(KT):
                        sp.wait_ge(attn_ready, KT * (UNITS * b - 1) + k + 1)
                        move_v(k)
                if has_a(b):
                    sp.wait_ge(scoresT_ready, PIECES * (UNITS * b + 2))
                    stack_pair(0)
                if has_o(b):
                    for q in range(2):
                        sp.wait_ge(y_ready, 2 * (b - 1) + q + 1)
                        store(b - 1, q)
                    if has_step(b, 0):
                        sp.wait_ge(stored, 2 * DMA * b)
                        load_resid(b)

            batches(sp, iteration)
            sp.wait_ge(stored, DMA * 2 * B)

        @block.tensor
        def _(pe):
            def task(t, n, bank, batch):
                kind = t[0]
                if kind == "ctxT":
                    pe.wait_ge(ctx_loaded, DMA * (batch + 1))
                    for k in range(DT):
                        last = nc.tensor.transpose(bank[:, KP * k:KP * k + KP], ctx_in[0:KP, t[1], P * k:P * k + P], ident[0:KP, 0:KP])
                elif kind == "xT":
                    pe.wait_ge(x_loaded, DMA * (batch + 1))
                    for k in range(DT):
                        last = nc.tensor.transpose(bank[:, QP * k:QP * k + QP], x_in[0:QP, t[1], P * k:P * k + P], ident[0:QP, 0:QP])
                elif kind == "W":
                    pe.wait_ge(w_loaded[t[1]], DMA)
                    for f in range(DT):
                        last = nc.tensor.transpose(bank[:, P * f:P * f + P], w_in[:, "qkvo".index(t[1]), f, P * t[2]:P * t[2] + P], ident[:])
                else:
                    first, n_mm = True, 3 * DT
                    for k in range(DT):
                        for a, c in ((0, 0), (0, 1), (1, 0)):
                            if kind == "K":
                                g, half = t[1], t[2]
                                dst, lhsT, rhs = bank[:, 0:KH], wT["k"][:, a, k, P * g:P * g + P], ctxT[:, c, k, KH * half:KH * half + KH]
                            elif kind == "Q":
                                g = t[1]
                                dst, lhsT, rhs = bank[:, 0:NQ], wT["q"][:, a, k, P * g:P * g + P], xT[:, c, k, :]
                            elif kind == "V":
                                i = t[1]
                                dst, lhsT, rhs = bank[0:KP, :], ctxT[:, a, k, KP * i:KP * i + KP], wT["v"][:, c, k, :]
                            else:
                                q = t[1]
                                dst, lhsT, rhs = bank[0:QP, :], attn_parts[:, a, k, QP * q:QP * q + QP], wT["o"][:, c, k, :]
                            n_mm -= 1
                            last = nc.tensor.matmul(dst, lhsT, rhs, start=first, stop=(n_mm == 0))
                            first = False
                last.then_inc(task_ready, 1)

            def scores(s, batch):
                g, h, q = s // UNIT, s % UNIT // 2, s % 2
                if s % (2 * UNIT) == 0:
                    pe.wait_ge(stacked[g // 2], DMA * STACK_DMAS * (batch + 1))
                for c in range(2):
                    last = nc.tensor.matmul(ps_scores[0:QP, 2 * (s % 2) + c, 0:KH],
                                            stacks[0:STACK_ROWS, g, h, NK + QP * q:NK + QP * q + QP],
                                            stacks[0:STACK_ROWS, g, h, KH * c:KH * c + KH], start=True, stop=True)
                last.then_inc(scores_ready, 1)

            def turn_maxima(u, g):
                pe.wait_ge(top_ready, UNIT * (u + 1))
                need(pe, probs_ready, PIECES * u - 1)
                for q in range(2):
                    last = nc.tensor.matmul(ps_scoresT[STACK_ROWS:STACK_ROWS + HG, 0, QP * q:QP * q + QP],
                                            top[0:QP, g % 2, q, :], ident[0:QP, 0:QP], start=True, stop=True,
                                            tile_position=(0, STACK_ROWS))
                last.then_inc(maxima_turned, 1)

            def scores_keymajor(u, g, piece):
                h, j = piece // 3, piece % 3
                if piece == 0:
                    pe.wait_ge(maxima_saved, u + 1)
                elif piece == 1:
                    need(pe, probs_ready, PIECES * u)
                else:
                    pe.wait_ge(probs_ready, PIECES * u + piece - 1)
                for i in range(2):
                    k = 2 * j + i
                    last = nc.tensor.matmul(ps_scoresT[0:KP, piece % 2, NQ * i:NQ * i + NQ],
                                            stacks[:, g, h, KP * k:KP * k + KP], stacks[:, g, h, Qc],
                                            start=True, stop=True)
                last.then_inc(scoresT_ready, 1)

            def attend(u, g, k, batch):
                if k == 0:
                    pe.wait_ge(probs_ready, PIECES * (u + 1))
                    need(pe, attn_scaled, u)
                if g == 0:
                    pe.wait_ge(v_moved[k], DMA * (batch + 1))
                for h in range(HG):
                    c = DK * h
                    last = nc.tensor.matmul(ps_attn[c:c + DK, 0:NQ], v_now[0:KP, k, P * g + c:P * g + c + DK],
                                            probsT[0:KP, g % 2, h, k, :], start=(k == 0), stop=(k == KT - 1),
                                            tile_position=(0, c))
                last.then_inc(attn_ready, 1)

            def sum_keys(u, g):
                pe.wait_ge(head_sums_ready, HG * (u + 1))
                for h in range(HG):
                    c = DK * h
                    last = nc.tensor.matmul(ps_attn[c:c + DK, SUMS:SUMS + NQ], ones[0:KP, :], head_sums[0:KP, g % 2, h, :],
                                            start=True, stop=True, tile_position=(0, c))
                last.then_inc(sums_ready, 1)

            pe.wait_ge(ident_ready, 1)
            for n, t in enumerate(prologue):
                if n >= PRO_BANKS:
                    pe.wait_ge(task_saved, n - PRO_BANKS + 1)
                if t[0] == "K" and t[1:] == (0, 0):
                    pe.wait_ge(task_saved, prologue.index(("W", "k", DT - 1)) + 1)
                if t == ("Q", 0):
                    pe.wait_ge(task_saved, prologue.index(("W", "q", DT - 1)) + 1)
                if t == ("V", 0):
                    pe.wait_ge(task_saved, prologue.index(("W", "v", DT - 1)) + 1)
                task(t, n, ps_scores[:, n % PRO_BANKS], 0)
            pe.wait_ge(task_saved, PRO)
            pe.wait_ge(pick_ready, 1)
            pe.wait_ge(ones_ready, 1)
            scores(0, 0)

            def iteration(b):
                tasks = iteration_tasks(b)
                before = tasks_before(b)
                for s in range(STEPS):
                    T = STEPS * b + s
                    g = s // UNIT
                    if has_step(b, s + 1):
                        need(pe, top_ready, T)
                        scores((s + 1) % STEPS, b if s < STEPS - 1 else b + 1)
                    u = unit_before(b, g, 1)
                    if u is not None:
                        if s % UNIT == 0:
                            turn_maxima(u, (g - 1) % UNITS)
                        for piece in pieces_of(s):
                            scores_keymajor(u, (g - 1) % UNITS, piece)
                    u = unit_before(b, g, 2)
                    if u is not None:
                        if s % UNIT >= 2:
                            attend(u, (g - 2) % UNITS, s % UNIT - 2, b if g >= 2 else b - 1)
                        if s % UNIT == UNIT - 1:
                            sum_keys(u, (g - 2) % UNITS)
                    if s in tasks:
                        t, place, _ = tasks[s]
                        pe.wait_ge(task_saved, before + place)
                        if t == ("O", 0):
                            pe.wait_ge(attn_low_saved, UNITS * b)
                        task(t, before + place, ps_task, b + 1)

            batches(pe, iteration)

        @block.scalar
        def _(act):
            def high_part(t, n, bank, batch):
                if t[0] not in SPLIT_KINDS:
                    return
                if t[0] in "KQ":
                    need(act, stacked[t[1] // 2], DMA * STACK_DMAS * batch)
                act.wait_ge(task_ready, n + 1)
                dst, src, b16 = split_views(t, bank, 0)
                if b16 is not None:
                    nc.scalar.activation(dst, src, ACT.Identity, bias=b16).then_inc(high_saved, 1)
                else:
                    nc.scalar.activation(dst, src, ACT.Copy, scale=WSCALE if t[0] == "W" else 1.0).then_inc(high_saved, 1)

            def save_maxima(u, g):
                act.wait_ge(maxima_turned, u + 1)
                nc.scalar.activation(stacks[STACK_ROWS:STACK_ROWS + HG, g, :, Qc],
                                     ps_scoresT[STACK_ROWS:STACK_ROWS + HG, 0:1, 0:NQ].broadcast_to([HG, HG, NQ]),
                                     ACT.Copy, scale=1.0 / MAX_SCALE).then_inc(maxima_saved, 1)

            def exp(u, g, piece):
                h, j = piece // 3, piece % 3
                act.wait_ge(scoresT_ready, PIECES * u + piece + 1)
                if piece == 0:
                    need(act, attn_ready, KT * (u - 1))
                    need(act, pair_sums_ready, HG * (u - 1))
                nc.scalar.activation(probsT[0:KP, g % 2, h, 2 * j:2 * j + 2, :].rearrange("p k q -> p (k q)"),
                                     ps_scoresT[0:KP, piece % 2, 0:2 * NQ], ACT.Exp, scale=SCORE_SCALE).then_inc(probs_ready, 1)

            def attn_high(u, g, task_n):
                act.wait_ge(attn_scaled, u + 1)
                if task_n is not None:
                    act.wait_ge(task_ready, task_n)
                nc.scalar.activation(attn_parts[:, 0, g, :], attn[:], ACT.Identity,
                                     bias=bias16["v"][:, g:g + 1]).then_inc(attn_high_saved, 1)

            act.wait_ge(bias_ready, 3)
            for n, t in enumerate(prologue):
                high_part(t, n, ps_scores[:, n % PRO_BANKS], 0)

            def iteration(b):
                tasks = iteration_tasks(b)
                before = tasks_before(b)
                for s in range(STEPS):
                    g = s // UNIT
                    if s - 1 in tasks:
                        t, place, _ = tasks[s - 1]
                        high_part(t, before + place, ps_task, b + 1)
                    u = unit_before(b, g, 1)
                    if u is not None:
                        if s % UNIT == 0:
                            save_maxima(u, (g - 1) % UNITS)
                        for piece in pieces_of(s):
                            exp(u, (g - 1) % UNITS, piece)
                    u = unit_before(b, g, 3)
                    if u is not None and s % UNIT == 1:
                        after_o = before + tasks[O_STEPS[1]][1] + 1 if g == 3 and has_o(b) else None
                        attn_high(u, (g - 3) % UNITS, after_o)

            batches(act, iteration)

        @block.vector
        def _(dve):
            def save_task(t, n, splits, bank, batch):
                kind = t[0]
                if kind in SPLIT_KINDS:
                    dst, src, b16 = split_views(t, bank, 1)
                    high = split_views(t, bank, 0)[0]
                    if kind in "KQ":
                        need(dve, stacked[t[1] // 2], DMA * STACK_DMAS * batch)
                    dve.wait_ge(high_saved, splits + 1)
                    if kind == "W":
                        nc.vector.scalar_tensor_tensor(dst, src, WSCALE, high, ALU.mult, ALU.subtract).then_inc(task_saved, 1)
                    elif b16 is not None:
                        nc.vector.scalar_tensor_tensor(dst, src, b16, high, ALU.add, ALU.subtract).then_inc(task_saved, 1)
                    else:
                        nc.vector.tensor_tensor(dst, src, high, ALU.subtract).then_inc(task_saved, 1)
                elif kind == "V":
                    dve.wait_ge(task_ready, n + 1)
                    need(dve, v_moved[t[1]], DMA * batch)
                    nc.vector.tensor_copy(v_next[0:KP, t[1]], bank[0:KP, :]).then_inc(task_saved, 1)
                else:
                    q = t[1]
                    dve.wait_ge(task_ready, n + 1)
                    if q == 0:
                        dve.wait_ge(resid_ready, 2 * (batch + 1))
                    nc.vector.scalar_tensor_tensor(y[0:QP, q], bank[0:QP, :], 1.0 / (WSCALE * WSCALE), resid[0:QP, q],
                                                   ALU.mult, ALU.add).then_inc(task_saved, 1)
                    dve.wait_ge(task_saved, n + 1)
                    nc.vector.bn_stats(stats[0:QP, q], y[0:QP, q]).then_inc(stats_ready, 1)

            def mean_of(q):
                nc.vector.bn_aggr(mean_var[0:QP, q], stats[0:QP, q]).then_inc(mean_ready, 1)

            def center(q, batch):
                dve.wait_ge(rstd_ready, 2 * batch + q + 1)
                nc.vector.tensor_scalar(y[0:QP, q], y[0:QP, q], mean_var[0:QP, q, 0:1], rstd[0:QP, q:q + 1],
                                        ALU.subtract, ALU.mult).then_inc(centered, 1)

            def row_max(s, T, unit):
                g, h, q = s // UNIT, s % UNIT // 2, s % 2
                dve.wait_ge(scores_ready, T + 1)
                if s % UNIT == 0:
                    need(dve, maxima_turned, unit - 1)
                nc.vector.tensor_reduce(top[0:QP, g % 2, q, h:h + 1], ps_scores[0:QP, 2 * (s % 2):2 * (s % 2) + 2, 0:KH],
                                        AX.XY, ALU.max).then_inc(top_ready, 1)

            def sum_head(u, g, h):
                dve.wait_ge(pair_sums_ready, HG * u + h + 1)
                if h == 0:
                    need(dve, sums_ready, u - 1)
                nc.vector.tensor_reduce(head_sums[0:KP, g % 2, h, :], pair_sums[0:KP, h % 2].rearrange("p k q -> p q k"),
                                        AX.X, ALU.add).then_inc(head_sums_ready, 1)

            def scale_attn(u):
                dve.wait_ge(sums_ready, u + 1)
                nc.vector.reciprocal(recip[:], ps_attn[:, SUMS:SUMS + NQ]).then_inc(recip_ready, 1)
                need(dve, attn_high_saved, u)
                need(dve, attn_low_saved, u)
                dve.wait_ge(recip_ready, u + 1)
                nc.vector.tensor_tensor(attn[:], ps_attn[:, 0:NQ], recip[:], ALU.mult).then_inc(attn_scaled, 1)

            def attn_low(u, g):
                dve.wait_ge(attn_high_saved, u + 1)
                nc.vector.scalar_tensor_tensor(attn_parts[:, 1, g, :], attn[:], bias16["v"][:, g:g + 1],
                                               attn_parts[:, 0, g, :], ALU.add, ALU.subtract).then_inc(attn_low_saved, 1)

            dve.wait_ge(bias_loaded, 3 * DMA)
            for w in "qkv":
                nc.vector.tensor_scalar(bias16[w][:], bias[w][:], WSCALE, None, ALU.mult).then_inc(bias_ready, 1)
            dve.wait_ge(bias_ready, 3)
            splits = 0
            for n, t in enumerate(prologue):
                save_task(t, n, splits, ps_scores[:, n % PRO_BANKS], 0)
                splits += t[0] in SPLIT_KINDS
            row_max(0, 0, 0)

            def iteration(b):
                tasks = iteration_tasks(b)
                before = tasks_before(b)
                for s in range(STEPS):
                    T = STEPS * b + s
                    g = s // UNIT
                    if s - 1 in tasks:
                        t, place, splits = tasks[s - 1]
                        save_task(t, before + place, splits_before(b) + splits, ps_task, b - 1 if t[0] == "O" else b + 1)
                    if has_o(b) and s - 1 in O_STEPS:
                        dve.wait_ge(stats_ready, 2 * (b - 1) + O_STEPS.index(s - 1) + 1)
                    if has_step(b, s + 1):
                        row_max((s + 1) % STEPS, T + 1, UNITS * b + (s + 1) // UNIT)
                    if has_o(b) and s - 1 in O_STEPS:
                        mean_of(O_STEPS.index(s - 1))
                    for back, i, h in ((1, 5, 0), (1, 6, 1), (2, 0, 2), (2, 1, 3)):
                        u = unit_before(b, g, back)
                        if u is not None and s % UNIT == i:
                            sum_head(u, (g - back) % UNITS, h)
                    u = unit_before(b, g, 3)
                    if u is not None:
                        if s % UNIT == 0:
                            scale_attn(u)
                        if s % UNIT == 2:
                            attn_low(u, (g - 3) % UNITS)
                    if has_o(b) and s - 3 in O_STEPS:
                        center(O_STEPS.index(s - 3), b - 1)

            batches(dve, iteration)

        @block.gpsimd
        def _(pool):
            nc.gpsimd.memset(ident[:], 0.0).then_inc(ident_zero, 1)
            pool.wait_ge(ident_zero, 1)
            nc.gpsimd.affine_select(out=ident[:], in_=ident[:], compare_op=ALU.not_equal, fill=1.0, base=0,
                                    pattern=[[-1, P]], channel_multiplier=1).then_inc(ident_ready, 1)
            nc.gpsimd.memset(ones[:], 1.0).then_inc(ones_ready, 1)
            nc.gpsimd.memset(eps[:], 1e-5).then_inc(const_ready, 1)
            nc.gpsimd.memset(minus_half[:], -0.5).then_inc(const_ready, 1)
            pool.wait_ge(const_ready, 2)
            nc.gpsimd.memset(stacks[STACK_ROWS:STACK_ROWS + HG, :, :, Kc], 0.0).then_inc(pick_zero, 1)
            pool.wait_ge(pick_zero, 1)
            for g in range(UNITS):
                k_rows = stacks[STACK_ROWS:STACK_ROWS + HG, g, :, Kc]
                last = nc.gpsimd.affine_select(out=k_rows, in_=k_rows, compare_op=ALU.not_equal, fill=-MAX_SCALE,
                                               base=0, pattern=[[-1, HG], [0, NK]], channel_multiplier=1)
            last.then_inc(pick_ready, 1)
            pool.wait_ge(pick_ready, 1)

            def sum_pairs(u, g, h):
                pool.wait_ge(probs_ready, PIECES * u + 3 * h + 3)
                need(pool, head_sums_ready, HG * u + h - 1)
                nc.gpsimd.tensor_tensor(pair_sums[0:KP, h % 2], probsT[0:KP, g % 2, h, 0:3, :], probsT[0:KP, g % 2, h, 3:6, :],
                                        ALU.add).then_inc(pair_sums_ready, 1)

            def add_bo(q, batch):
                if q == 0:
                    pool.wait_ge(resid_loaded, DMA * (batch + 1))
                nc.gpsimd.tensor_tensor(resid[0:QP, q], resid[0:QP, q], rows["bo"][0:QP], ALU.add).then_inc(resid_ready, 1)

            def rstd_of(q, batch):
                pool.wait_ge(mean_ready, 2 * batch + q + 1)
                nc.gpsimd.tensor_tensor(var_eps[0:QP, q:q + 1], mean_var[0:QP, q, 1:2], eps[0:QP], ALU.add).then_inc(var_eps_ready, 1)
                pool.wait_ge(var_eps_ready, 2 * batch + q + 1)
                nc.gpsimd.tensor_tensor(rstd[0:QP, q:q + 1], var_eps[0:QP, q:q + 1], minus_half[0:QP], ALU.pow).then_inc(rstd_ready, 1)

            def times_gamma(q, batch):
                pool.wait_ge(centered, 2 * batch + q + 1)
                nc.gpsimd.tensor_tensor(y[0:QP, q], y[0:QP, q], rows["gamma"][0:QP], ALU.mult).then_inc(y_scaled, 1)

            def plus_beta(q, batch):
                pool.wait_ge(y_scaled, 2 * batch + q + 1)
                nc.gpsimd.tensor_tensor(y[0:QP, q], y[0:QP, q], rows["beta"][0:QP], ALU.add).then_inc(y_ready, 1)

            pool.wait_ge(rows_loaded, 3 * DMA)

            def iteration(b):
                for s in range(STEPS):
                    g = s // UNIT
                    for back, i, h in ((1, 4, 0), (1, 5, 1), (1, 7, 2), (2, 0, 3)):
                        u = unit_before(b, g, back)
                        if u is not None and s % UNIT == i:
                            sum_pairs(u, (g - back) % UNITS, h)
                    if has_o(b):
                        for q in range(2):
                            if s == 9 + q:
                                add_bo(q, b - 1)
                            if s == O_STEPS[q] + 1:
                                rstd_of(q, b - 1)
                            if s == O_STEPS[q] + 3:
                                times_gamma(q, b - 1)
                            if s == O_STEPS[q] + 4:
                                plus_beta(q, b - 1)

            batches(pool, iteration)


_INS = ["x", "ctx_1024", "L0_xattn_Wq", "L0_xattn_bq", "L0_xattn_Wk", "L0_xattn_bk", "L0_xattn_Wv", "L0_xattn_bv",
        "L0_xattn_Wo", "L0_xattn_bo", "L0_xattn_gamma", "L0_xattn_beta"]


def kernel(**inputs):
    import numpy as np
    import concourse.bacc as bacc
    from concourse.bass_utils import run_bass_kernel_spmd

    nc = bacc.Bacc("TRN2", target_bir_lowering=False, num_devices=1)
    arrays, args = {}, []
    for name in _INS:
        a = np.ascontiguousarray(inputs[name])
        arrays[f"in_{name}"] = a
        args.append(nc.dram_tensor(f"in_{name}", a.shape, mybir.dt.from_np(a.dtype), kind="ExternalInput").ap())
    result = nc.dram_tensor("out_y", inputs["x"].shape, F32, kind="ExternalOutput").ap()
    build(nc, *args, result)
    r = run_bass_kernel_spmd(nc, [arrays], core_ids=[0])
    return r.results[0]["out_y"]
```

```python
from contextlib import ExitStack

import concourse.bass as bass
from concourse import mybir

F32 = mybir.dt.float32
F16 = mybir.dt.float16
ALU = mybir.AluOpType
ACT = mybir.ActivationFunctionType
AX = mybir.AxisListType

WSCALE = 16.0
DMA = 16


def build(nc, x, ctx_tokens, Wq, bq, Wk, bk, Wv, bv, Wo, bo, gamma, beta, out):
    B, NQ, D = x.shape
    NK = ctx_tokens.shape[1]
    HEADS = 16
    DK = D // HEADS
    P = 128
    DT = D // P
    QP = NQ // 2
    KT = 6
    KP = NK // KT
    KH = NK // 2
    HG = P // DK
    UNITS = HEADS // HG
    UNIT = 2 * HG
    STEPS = UNIT * UNITS
    LAST = B - 1
    SCORE_SCALE = 1.0 / (WSCALE * WSCALE * float(DK) ** 0.5)
    SPLIT_ROWS = ((0, 0), (1, 0), (0, 1))
    STACK_ROWS = DK * len(SPLIT_ROWS)
    STACK_DMAS = 4
    HALVES = 2 * STEPS
    RING = 3
    BANK = [i % RING for i in range(HALVES)]
    BANK[-1] = 1
    PIECES = 3 * HG
    WARM_UP = 8
    MAX_SCALE = 1024.0
    NU = B * UNITS
    VECTOR_HEADS = (HG * (NU - 1) - 2, HG * (NU - 1) - 1)
    assert QP * 2 == NQ and KP * KT == NK and UNITS % 2 == 0 and STACK_ROWS + HG <= P and KT == 6

    OWN = {0: ("K", 2, 0), 1: ("V", 0), 2: ("K", 2, 1), 3: ("Q", 2), 4: ("K", 3, 0), 5: ("V", 1), 8: ("K", 3, 1),
           9: ("V", 2), 11: ("V", 3), 12: ("Q", 3), 14: ("V", 4), 17: ("V", 5)}
    NEXT = {6: ("ctxT", 0), 10: ("ctxT", 1), 13: ("ctxT", 2), 15: ("K", 0, 0), 16: ("K", 1, 0), 18: ("ctxT", 3),
            19: ("ctxT", 4), 20: ("xT", 0), 21: ("ctxT", 5), 22: ("xT", 1), 23: ("K", 0, 1), 25: ("Q", 0),
            27: ("K", 1, 1), 29: ("Q", 1)}
    OUTPUT = {24: ("O", 0), 26: ("O", 1)}
    assert all(len(t) % 2 == 0 for t in (OWN, NEXT, OUTPUT))
    assert not OWN.keys() & NEXT.keys() and not (OWN.keys() | NEXT.keys()) & OUTPUT.keys()
    O_STEPS = sorted(OUTPUT)
    STAGES = {**{("attend", k): (2, 2 + k) for k in range(KT)}, "sum_keys": (2, 7), "copy": (3, 0), ("invert", 0): (3, 1),
              ("invert", 1): (3, 2), "scale": (3, 3), "high": (3, 4), "low": (3, 5)}
    TAIL = {NU - 3: {"copy": 0, ("invert", 0): 1, ("invert", 1): 2, "scale": 3, "high": 4, "low": 5},
            NU - 2: {**{("attend", k): max(k, 1) for k in range(KT)}, "sum_keys": 5, "copy": 6, ("invert", 0): 7, ("invert", 1): 8,
                     "scale": 9, "high": 10, "low": 10},
            NU - 1: {"copy": 11, ("invert", 0): 12, ("invert", 1): 13, "scale": 14, "high": 15, "low": 16}}
    HIGH_STEP, LOW_STEP = STAGES["high"][1], STAGES["low"][1]
    SUM_STEPS = ((1, 4, 0), (1, 5, 1), (1, 7, 2), (2, 0, 3))
    assert 2 * UNIT + LOW_STEP < O_STEPS[0] and O_STEPS[1] < 3 * UNIT + HIGH_STEP
    LAST_USE = UNIT + 2
    STEP_OF = {t: s for s, t in {**OWN, **NEXT, **OUTPUT}.items()}
    SPLIT_KINDS = ("ctxT", "xT", "K", "Q", "W")
    prologue = ([("xT", 0), ("xT", 1)] + [("ctxT", i) for i in range(3)] + [("W", "k", k) for k in range(DT)]
                + [("ctxT", i) for i in range(3, KT)] + [("K", 0, 0), ("W", "q", 0), ("W", "q", 1), ("K", 0, 1),
                   ("W", "q", 2), ("W", "q", 3), ("K", 1, 0), ("Q", 0), ("W", "v", 0), ("W", "v", 1), ("W", "v", 2), ("W", "v", 3),
                   ("K", 1, 1), ("W", "o", 0), ("W", "o", 1), ("W", "o", 2), ("W", "o", 3), ("Q", 1)])
    PRO = len(prologue)
    PRO_BIASES = prologue.index(("K", 0, 0))

    def tasks_of(b):
        known = isinstance(b, int)
        found = dict(OWN) if not known or b < B else {}
        found.update(NEXT if not known or b < LAST else {})
        found.update(OUTPUT if not known or b > 0 else {})
        return found

    def is_last(u):
        return isinstance(u, int) and u == NU - 1

    def vector_sums(n):
        return isinstance(n, int) and n in VECTOR_HEADS

    def sums_on_gpsimd(n):
        return n - sum(i < n for i in VECTOR_HEADS) if isinstance(n, int) else n

    def has_next(b):
        return NEXT.items() <= tasks_of(b).items()

    def has_output(b):
        return OUTPUT.items() <= tasks_of(b).items()

    def iteration_tasks(b):
        found, splits = {}, 0
        for place, (s, t) in enumerate(sorted(tasks_of(b).items())):
            found[s] = (t, place, splits)
            splits += t[0] in SPLIT_KINDS
        return found

    def tasks_before(b):
        if isinstance(b, int):
            return PRO + sum(len(tasks_of(i)) for i in range(b))
        return PRO - len(OUTPUT) + (len(OWN) + len(NEXT) + len(OUTPUT)) * b

    def splits_before(b):
        return len([t for t in prologue if t[0] in SPLIT_KINDS]) + len([t for t in {**OWN, **NEXT}.values() if t[0] in SPLIT_KINDS]) * b

    def inputs_of(t):
        if t not in NEXT.values() or t[0] not in "KQ":
            return []
        return [("xT", 0), ("xT", 1)] if t[0] == "Q" else [("ctxT", i) for i in range(3 * t[2], 3 * t[2] + 3)]

    def batch_of(t, s, b):
        return b - 1 if s in OUTPUT else b + 1 if s in NEXT else b

    with ExitStack() as stack:
        def sb(name, shape, dt=F32):
            return stack.enter_context(nc.sbuf_tensor(name, shape, dt))

        def psum(name, shape):
            return stack.enter_context(nc.psum_tensor(name, shape, F32))

        def sem(name):
            return stack.enter_context(nc.semaphore(name))

        ps_scores = psum("ps_scores", [P, RING, 512])
        ps_scoresT = psum("ps_scoresT", [P, 2, 512])
        ps_attn = psum("ps_attn", [P, 512])
        ps_task = psum("ps_task", [P, 2, 512])
        pro_banks = [ps_scores[:, i] for i in range(RING)] + [ps_task[:, i] for i in range(2)]
        PRO_BANKS = len(pro_banks)
        SUMS = 256

        wT = {w: sb(f"w{w}T", [P, 2, DT, D], F16) for w in "qkvo"}
        ctx_in = sb("ctx_in", [P, KT, D])
        x_in = sb("x_in", [P, 2, D])
        ctxT = sb("ctxT", [P, 2, DT, NK], F16)
        xT = sb("xT", [P, 2, DT, NQ], F16)
        KQ = NK + NQ
        Kc, Qc = slice(0, NK), slice(NK, KQ)
        parts = sb("parts", [P, UNITS, 2, KQ], F16)
        stacks = sb("stacks", [STACK_ROWS + HG, UNITS, HG, KQ], F16)
        v_next = sb("v_next", [P, KT, D])
        v_now = sb("v_now", [P, KT, D])
        probsT = sb("probsT", [P, 2, HG, KT, NQ])
        w_in = probsT[:].rearrange("p u h k q -> p (u h k q)")[:, 0:4 * DT * D].rearrange(
            "p (w t d) -> p w t d", w=4, t=DT)
        top_halves = sb("top_halves", [P, 2, 2, HG, 2])
        top = sb("top", [P, 2, 2, HG])
        pair_sums = sb("pair_sums", [P, 3, NQ])
        head_sums = sb("head_sums", [P, 2, HG, NQ])
        ones = sb("ones", [P, DK])
        recip = sb("recip", [P, NQ])
        attn_sums = sb("attn_sums", [P, 2, NQ])
        attn = sb("attn", [P, NQ])
        attn_parts = sb("attn_parts", [P, 2, UNITS, NQ], F16)
        resid = sb("resid", [P, 2, D])
        y = sb("y", [P, 2, D])
        stats = sb("stats", [P, 2, 6])
        mean_var = sb("mean_var", [P, 2, 2])
        var_eps = sb("var_eps", [P, 2])
        rstd = sb("rstd", [P, 2])
        eps = sb("eps", [P, 1])
        minus_half = sb("minus_half", [P, 1])
        bias = {w: sb(f"b{w}_in", [P, DT]) for w in "qkv"}
        bias16 = {w: sb(f"b{w}16", [P, DT]) for w in "qkv"}
        rows = {n: sb(f"{n}_row", [P, D]) for n in ("gamma", "beta", "bo")}
        ident = sb("ident", [P, P])

        ctx_half_loaded, ctx_loaded, x_loaded = sem("ctx_half_loaded"), sem("ctx_loaded"), sem("x_loaded")
        w_loaded = {w: sem(f"w{w}_loaded") for w in "qkvo"}
        bias_loaded, rows_loaded = sem("bias_loaded"), sem("rows_loaded")
        resid_loaded = sem("resid_loaded")
        stacked = [[sem(f"stacked{g}_{h}") for h in range(HG)] for g in range(UNITS)]
        v_moved = [sem(f"v_moved{k}") for k in range(KT)]
        stored = sem("stored")
        scores_ready, maxima_turned, scoresT_ready = sem("scores_ready"), sem("maxima_turned"), sem("scoresT_ready")
        task_ready, attn_ready, sums_ready = sem("task_ready"), sem("attn_ready"), sem("sums_ready")
        maxima_saved, probs_ready, attn_copied = sem("maxima_saved"), sem("probs_ready"), sem("attn_copied")
        high_saved, attn_high_saved = sem("high_saved"), sem("attn_high_saved")
        half_top_ready, top_ready, task_saved = sem("half_top_ready"), sem("top_ready"), sem("task_saved")
        recip_ready, attn_scaled, attn_low_saved = sem("recip_ready"), sem("attn_scaled"), sem("attn_low_saved")
        last_sums_ready, last_scaled, last_ready = sem("last_sums_ready"), sem("last_scaled"), sem("last_ready")
        stats_ready, mean_ready, centered, bias_ready = sem("stats_ready"), sem("mean_ready"), sem("centered"), sem("bias_ready")
        ones_ready, ident_zero, ident_ready = sem("ones_ready"), sem("ident_zero"), sem("ident_ready")
        pick_zero, pick_ready = sem("pick_zero"), sem("pick_ready")
        pair_sums_ready, two_sums_ready, head_sums_ready = sem("pair_sums_ready"), sem("two_sums_ready"), sem("head_sums_ready")
        const_ready, resid_ready, var_eps_ready, rstd_ready = sem("const_ready"), sem("resid_ready"), sem("var_eps_ready"), sem("rstd_ready")
        y_scaled, y_ready = sem("y_scaled"), sem("y_ready")

        def need(eng, s, value):
            if not isinstance(value, int) or value > 0:
                eng.wait_ge(s, value)

        def dram(t, b):
            return t[b] if isinstance(b, int) else t[bass.ds(b, 1)].rearrange("a t d -> (a t) d")

        def batches(eng, iteration):
            iteration(0)
            with eng.Fori(1, LAST - 1) as b:
                iteration(b)
            iteration(LAST - 1)
            iteration(LAST)
            iteration(B)

        def unit_before(b, g, back):
            u = UNITS * b + g - back
            return u if not isinstance(u, int) or 0 <= u < NU else None

        def due(stage, b, s):
            if isinstance(b, int) and b == B:
                return [(u, u % UNITS) for u in TAIL if TAIL[u].get(stage) == s]
            back, at = STAGES[stage]
            u = unit_before(b, s // UNIT, back)
            return [(u, (s // UNIT - back) % UNITS)] if s % UNIT == at and u is not None else []

        def head_and_tiles(u, piece):
            if is_last(u):
                return piece % HG, piece // HG
            return piece // 3, piece % 3

        def has_step(b, s):
            return not isinstance(b, int) or 0 <= STEPS * b + s < STEPS * B

        def pieces_of(s):
            i = s % UNIT
            return (2 * i - 4, 2 * i - 3) if i >= 2 else ()

        def split_views(t, bank, part):
            kind = t[0]
            if kind == "ctxT":
                i = t[1]
                return ctxT[:, part, :, KP * i:KP * i + KP], bank[:, 0:DT * KP].rearrange("p (k t) -> p k t", k=DT), None
            if kind == "xT":
                i = t[1]
                return xT[:, part, :, QP * i:QP * i + QP], bank[:, 0:DT * QP].rearrange("p (k t) -> p k t", k=DT), None
            if kind == "W":
                return wT[t[1]][:, part, t[2], :], bank[:, :], None
            g = t[1]
            if kind == "K":
                return parts[:, g, part, KH * t[2]:KH * t[2] + KH], bank[:, 0:KH], bias16["k"][:, g:g + 1]
            return parts[:, g, 1 - part, Qc], bank[:, 0:NQ], bias16["q"][:, g:g + 1]

        block = stack.enter_context(nc.Block())

        @block.sync
        def _(sp):
            def load_ctx(b):
                sp.dma_start(ctx_in[0:KP], dram(ctx_tokens, b).rearrange("(k p) d -> p k d", p=KP)).then_inc(ctx_loaded, DMA)

            def load_x(b):
                sp.dma_start(x_in[0:QP], dram(x, b).rearrange("(q p) d -> p q d", p=QP)).then_inc(x_loaded, DMA)

            def load_resid(b):
                sp.dma_start(resid[0:QP], dram(x, b).rearrange("(q p) d -> p q d", p=QP)).then_inc(resid_loaded, DMA)

            def fill_stack(g):
                for h in range(HG):
                    rows_of_h = slice(DK * h, DK * h + DK)
                    for r, (q_part, k_part) in enumerate(SPLIT_ROWS):
                        to = slice(DK * r, DK * r + DK)
                        if q_part != k_part:
                            sp.dma_start(stacks[to, g, h, :], parts[rows_of_h, g, k_part, :]).then_inc(stacked[g][h], DMA)
                        else:
                            sp.dma_start(stacks[to, g, h, Kc], parts[rows_of_h, g, k_part, Kc]).then_inc(stacked[g][h], DMA)
                            sp.dma_start(stacks[to, g, h, Qc], parts[rows_of_h, g, 1 - q_part, Qc]).then_inc(stacked[g][h], DMA)

            def move_v(k):
                sp.dma_start(v_now[0:KP, k], v_next[0:KP, k]).then_inc(v_moved[k], DMA)

            def store(b, q):
                sp.dma_start(dram(out, b).rearrange("(q p) d -> p q d", p=QP)[:, q], y[0:QP, q]).then_inc(stored, DMA)

            def load_w(w, W):
                sp.dma_start(w_in[:, "qkvo".index(w)], W.rearrange("(t p) d -> p t d", p=P)).then_inc(w_loaded[w], DMA)

            load_x(0)
            first = ctx_tokens[0].rearrange("(k p) d -> p k d", p=KP)
            sp.dma_start(ctx_in[0:KP, 0:KT // 2], first[:, 0:KT // 2]).then_inc(ctx_half_loaded, DMA)
            load_w("k", Wk)
            sp.dma_start(ctx_in[0:KP, KT // 2:KT], first[:, KT // 2:KT]).then_inc(ctx_loaded, DMA)
            for name, v in (("k", bk), ("q", bq), ("v", bv)):
                sp.dma_start(bias[name][:], v.rearrange("(t p) -> p t", p=P), allow_slow_non_contiguous=True).then_inc(bias_loaded, DMA)
            load_w("q", Wq)
            load_w("v", Wv)
            load_w("o", Wo)
            for name, v in (("gamma", gamma), ("beta", beta), ("bo", bo)):
                sp.dma_start(rows[name][0:QP], v.partition_broadcast(QP)).then_inc(rows_loaded, DMA)
            sp.wait_ge(task_ready, prologue.index(("ctxT", KT - 1)) + 1)
            load_x(1)
            load_ctx(1)
            for g in range(2):
                sp.wait_ge(task_saved, prologue.index(("Q", g)) + 1)
                fill_stack(g)
            load_resid(0)

            def iteration(b):
                tasks = iteration_tasks(b)
                before = tasks_before(b)

                def after(*kinds):
                    return before + max(tasks[STEP_OF[t]][1] for t in kinds) + 1

                if 0 in tasks:
                    def fill(g):
                        sp.wait_ge(task_saved, after(("K", g, 0), ("K", g, 1), ("Q", g)))
                        fill_stack(g)

                    def move(k):
                        if isinstance(b, int):
                            need(sp, attn_ready, KT * (UNITS * b - 1) + k + 1)
                            sp.wait_ge(task_saved, after(("V", k)))
                        else:
                            s = min(s for s in tasks if s >= max(STEP_OF["V", k], LAST_USE + k))
                            sp.wait_ge(task_saved, before + tasks[s][1] + 1)
                        move_v(k)

                    fill(2)
                    for k in range(4):
                        move(k)
                    fill(3)
                    for k in range(4, KT):
                        move(k)
                if has_next(b):
                    if not (isinstance(b, int) and b == LAST - 1):
                        sp.wait_ge(task_ready, after(*[("ctxT", i) for i in range(KT)]))
                        load_ctx(b + 2)
                        sp.wait_ge(task_ready, after(("xT", 0), ("xT", 1)))
                        load_x(b + 2)
                    sp.wait_ge(task_saved, after(("K", 0, 0), ("K", 0, 1), ("Q", 0)))
                    fill_stack(0)
                if has_output(b):
                    for q in range(2):
                        if q == 1 and isinstance(b, int) and b == B:
                            sp.wait_ge(last_ready, 1)
                        else:
                            sp.wait_ge(y_ready, 2 * (b - 1) + q + 1)
                        store(b - 1, q)
                    if has_step(b, 0):
                        sp.wait_ge(stored, 2 * DMA * b)
                        load_resid(b)
                if has_next(b):
                    sp.wait_ge(task_saved, after(("K", 1, 0), ("K", 1, 1), ("Q", 1)))
                    fill_stack(1)

            batches(sp, iteration)
            sp.wait_ge(stored, DMA * 2 * B)

        @block.tensor
        def _(pe):
            def project_output(q, bank, tiles, batch):
                for k in tiles:
                    if k == 0:
                        pe.wait_ge(attn_low_saved, UNITS * batch + UNITS - 1)
                    if k == UNITS - 1:
                        pe.wait_ge(attn_low_saved, UNITS * batch + UNITS)
                    for a, c in ((0, 0), (0, 1), (1, 0)):
                        last = nc.tensor.matmul(bank[0:QP, :], attn_parts[:, a, k, QP * q:QP * q + QP], wT["o"][:, c, k, :],
                                                start=(k == 0 and (a, c) == (0, 0)), stop=(k == UNITS - 1 and (a, c) == (1, 0)))
                return last

            def task(t, n, bank, batch):
                kind = t[0]
                if kind == "ctxT":
                    if isinstance(batch, int) and batch == 0 and t[1] < KT // 2:
                        pe.wait_ge(ctx_half_loaded, DMA)
                    else:
                        pe.wait_ge(ctx_loaded, DMA * (batch + 1))
                    for k in range(DT):
                        last = nc.tensor.transpose(bank[:, KP * k:KP * k + KP], ctx_in[0:KP, t[1], P * k:P * k + P], ident[0:KP, 0:KP])
                elif kind == "xT":
                    pe.wait_ge(x_loaded, DMA * (batch + 1))
                    for k in range(DT):
                        last = nc.tensor.transpose(bank[:, QP * k:QP * k + QP], x_in[0:QP, t[1], P * k:P * k + P], ident[0:QP, 0:QP])
                elif kind == "W":
                    pe.wait_ge(w_loaded[t[1]], DMA)
                    for f in range(DT):
                        last = nc.tensor.transpose(bank[:, P * f:P * f + P], w_in[:, "qkvo".index(t[1]), f, P * t[2]:P * t[2] + P], ident[:])
                elif kind == "O":
                    last = project_output(t[1], bank, range(UNITS), batch)
                else:
                    first, n_mm = True, 3 * DT
                    for k in range(DT):
                        for a, c in ((0, 0), (0, 1), (1, 0)):
                            if kind == "K":
                                g, half = t[1], t[2]
                                dst, lhsT, rhs = bank[:, 0:KH], wT["k"][:, a, k, P * g:P * g + P], ctxT[:, c, k, KH * half:KH * half + KH]
                            elif kind == "Q":
                                g = t[1]
                                dst, lhsT, rhs = bank[:, 0:NQ], wT["q"][:, a, k, P * g:P * g + P], xT[:, c, k, :]
                            else:
                                i = t[1]
                                dst, lhsT, rhs = bank[0:KP, :], ctxT[:, a, k, KP * i:KP * i + KP], wT["v"][:, c, k, :]
                            n_mm -= 1
                            last = nc.tensor.matmul(dst, lhsT, rhs, start=first, stop=(n_mm == 0))
                            first = False
                last.then_inc(task_ready, 1)

            def scores(s, batch):
                g, h, q = s // UNIT, s % UNIT // 2, s % 2
                if q == 0:
                    pe.wait_ge(stacked[g][h], DMA * STACK_DMAS * (batch + 1))
                for c in range(2):
                    i = 2 * s + c
                    before = max(j for j in range(-HALVES, i) if BANK[j % HALVES] == BANK[i])
                    need(pe, half_top_ready, HALVES * batch + before + 1)
                    nc.tensor.matmul(ps_scores[0:QP, BANK[i], 0:KH],
                                     stacks[0:STACK_ROWS, g, h, NK + QP * q:NK + QP * q + QP],
                                     stacks[0:STACK_ROWS, g, h, KH * c:KH * c + KH], start=True, stop=True).then_inc(scores_ready, 1)

            def turn_maxima(u, g):
                pe.wait_ge(top_ready, u + 1)
                need(pe, probs_ready, PIECES * u - 1)
                for q in range(2):
                    last = nc.tensor.matmul(ps_scoresT[STACK_ROWS:STACK_ROWS + HG, 0, QP * q:QP * q + QP],
                                            top[0:QP, g % 2, q, :], ident[0:QP, 0:QP], start=True, stop=True,
                                            tile_position=(0, STACK_ROWS))
                last.then_inc(maxima_turned, 1)

            def scores_keymajor(u, g, piece):
                h, j = head_and_tiles(u, piece)
                if piece == 0:
                    pe.wait_ge(maxima_saved, u + 1)
                elif piece == 1:
                    need(pe, probs_ready, PIECES * u)
                else:
                    pe.wait_ge(probs_ready, PIECES * u + piece - 1)
                for i in range(2):
                    k = 2 * j + i
                    last = nc.tensor.matmul(ps_scoresT[0:KP, piece % 2, NQ * i:NQ * i + NQ],
                                            stacks[:, g, h, KP * k:KP * k + KP], stacks[:, g, h, Qc],
                                            start=True, stop=True)
                last.then_inc(scoresT_ready, 1)

            def attend(u, g, k, batch):
                if k == 0:
                    pe.wait_ge(probs_ready, PIECES * (u + 1))
                    need(pe, attn_copied, u)
                if g == 0:
                    pe.wait_ge(v_moved[k], DMA * (batch + 1))
                for h in range(HG):
                    c = DK * h
                    last = nc.tensor.matmul(ps_attn[c:c + DK, 0:NQ], v_now[0:KP, k, P * g + c:P * g + c + DK],
                                            probsT[0:KP, g % 2, h, k, :], start=(k == 0), stop=(k == KT - 1),
                                            tile_position=(0, c))
                last.then_inc(attn_ready, 1)

            def attend_last(k):
                u, g = NU - 1, UNITS - 1
                pe.wait_ge(probs_ready, PIECES * u + HG * (k // 2 + 1))
                for bank, signal in ((1, attn_ready), (2, sums_ready)):
                    for h in range(HG):
                        c = DK * h
                        last = nc.tensor.matmul(ps_scores[c:c + DK, bank, 0:NQ],
                                                v_now[0:KP, k, P * g + c:P * g + c + DK] if bank == 1 else ones[0:KP, :],
                                                probsT[0:KP, g % 2, h, k, :], start=(k == 0), stop=(k == KT - 1),
                                                tile_position=(0, c))
                    if bank == 1 or k == KT - 1:
                        last.then_inc(signal, 1)

            def sum_keys(u, g):
                pe.wait_ge(head_sums_ready, sums_on_gpsimd(HG * (u + 1)))
                if isinstance(u, int):
                    need(pe, last_sums_ready, sum(n < HG * (u + 1) for n in VECTOR_HEADS))
                for h in range(HG):
                    c = DK * h
                    last = nc.tensor.matmul(ps_attn[c:c + DK, SUMS:SUMS + NQ], ones[0:KP, :], head_sums[0:KP, g % 2, h, :],
                                            start=True, stop=True, tile_position=(0, c))
                last.then_inc(sums_ready, 1)

            pe.wait_ge(ident_ready, 1)
            for _ in range(WARM_UP):
                nc.tensor.matmul(ps_attn[:, 0:P], ident[:], ident[:], start=True, stop=True)
            for n, t in enumerate(prologue):
                if n >= PRO_BANKS:
                    pe.wait_ge(task_saved, n - PRO_BANKS + 1)
                if t[0] in "KQ":
                    own = [("xT", 1)] if t[0] == "Q" else [("ctxT", 3 * t[2] + 2)]
                    pe.wait_ge(task_saved, max(prologue.index(i) for i in own + [("W", t[0].lower(), DT - 1)]) + 1)
                task(t, n, pro_banks[n % PRO_BANKS], 0)
            pe.wait_ge(task_saved, max(n for n in range(PRO) if n % PRO_BANKS < RING) + 1)
            pe.wait_ge(pick_ready, 1)
            pe.wait_ge(ones_ready, 1)
            scores(0, 0)

            def iteration(b):
                tasks = iteration_tasks(b)
                before = tasks_before(b)
                for s in range(STEPS):
                    g = s // UNIT
                    if has_step(b, s + 1):
                        scores((s + 1) % STEPS, b if s < STEPS - 1 else b + 1)
                    u = unit_before(b, g, 1)
                    if u is not None:
                        if s % UNIT == 0:
                            turn_maxima(u, (g - 1) % UNITS)
                        for piece in pieces_of(s):
                            scores_keymajor(u, (g - 1) % UNITS, piece)
                    for k in range(KT):
                        for u, g_u in due(("attend", k), b, s):
                            attend(u, g_u, k, b if g >= 2 else b - 1)
                    for u, g_u in due("sum_keys", b, s):
                        sum_keys(u, g_u)
                    if isinstance(b, int) and b == B:
                        for k in range(KT):
                            if s == 4 + k:
                                attend_last(k)
                    if s in tasks:
                        t, place, _ = tasks[s]
                        pe.wait_ge(task_saved, before + max([place - 1] + [tasks[STEP_OF[i]][1] + 1 for i in inputs_of(t)]))
                        if isinstance(b, int) and b == B:
                            project_output(t[1], ps_task[:, place % 2], [UNITS - 1], b - 1).then_inc(task_ready, 1)
                        else:
                            task(t, before + place, ps_task[:, place % 2], batch_of(t, s, b))
                    if isinstance(b, int) and b == B and s == 2 * UNIT - 1:
                        pe.wait_ge(task_saved, before)
                        for t, place, _ in tasks.values():
                            project_output(t[1], ps_task[:, place % 2], range(UNITS - 1), b - 1)

            batches(pe, iteration)

        @block.scalar
        def _(act):
            def high_part(t, n, bank):
                if t[0] not in SPLIT_KINDS:
                    return
                act.wait_ge(task_ready, n + 1)
                dst, src, b16 = split_views(t, bank, 0)
                if b16 is not None:
                    nc.scalar.activation(dst, src, ACT.Identity, bias=b16).then_inc(high_saved, 1)
                else:
                    nc.scalar.activation(dst, src, ACT.Copy, scale=WSCALE if t[0] == "W" else 1.0).then_inc(high_saved, 1)

            def save_maxima(u, g):
                act.wait_ge(maxima_turned, u + 1)
                nc.scalar.activation(stacks[STACK_ROWS:STACK_ROWS + HG, g, :, Qc],
                                     ps_scoresT[STACK_ROWS:STACK_ROWS + HG, 0:1, 0:NQ].broadcast_to([HG, HG, NQ]),
                                     ACT.Copy, scale=1.0 / MAX_SCALE).then_inc(maxima_saved, 1)

            def exp(u, g, piece):
                h, j = head_and_tiles(u, piece)
                act.wait_ge(scoresT_ready, PIECES * u + piece + 1)
                if piece == 0:
                    need(act, attn_ready, KT * (u - 1))
                    need(act, pair_sums_ready, HG * (u - 1))
                nc.scalar.activation(probsT[0:KP, g % 2, h, 2 * j:2 * j + 2, :].rearrange("p k q -> p (k q)"),
                                     ps_scoresT[0:KP, piece % 2, 0:2 * NQ], ACT.Exp, scale=SCORE_SCALE).then_inc(probs_ready, 1)

            def copy_attn(u):
                act.wait_ge(sums_ready, u + 1)
                need(act, attn_scaled, u)
                source = ps_attn[:].rearrange("p (a q) -> p a q", a=2) if not is_last(u) else ps_scores[:, 1:3]
                nc.scalar.copy(attn_sums[:], source[:, :, 0:NQ]).then_inc(attn_copied, 1)

            def attn_high(u, g, task_n):
                act.wait_ge(attn_scaled, u + 1)
                if task_n is not None:
                    act.wait_ge(task_ready, task_n)
                nc.scalar.activation(attn_parts[:, 0, g, :], attn[:], ACT.Identity,
                                     bias=bias16["v"][:, g:g + 1]).then_inc(attn_high_saved, 1)

            for n, t in enumerate(prologue):
                if n == PRO_BIASES:
                    act.wait_ge(bias_ready, 3)
                high_part(t, n, pro_banks[n % PRO_BANKS])

            def iteration(b):
                tasks = iteration_tasks(b)
                before = tasks_before(b)
                for s in range(STEPS):
                    g = s // UNIT
                    if s - 1 in tasks:
                        t, place, _ = tasks[s - 1]
                        high_part(t, before + place, ps_task[:, place % 2])
                    for u, _ in due("copy", b, s):
                        copy_attn(u)
                    u = unit_before(b, g, 1)
                    if u is not None:
                        if s % UNIT == 0:
                            save_maxima(u, (g - 1) % UNITS)
                        for piece in pieces_of(s):
                            exp(u, (g - 1) % UNITS, piece)
                    for u, g_u in due("high", b, s):
                        after_o = before + tasks[O_STEPS[1]][1] + 1 if g_u == 0 and has_output(b) else None
                        attn_high(u, g_u, after_o)

            batches(act, iteration)

        @block.vector
        def _(dve):
            def save_task(t, n, splits, bank, batch):
                kind = t[0]
                if kind in SPLIT_KINDS:
                    dst, src, b16 = split_views(t, bank, 1)
                    high = split_views(t, bank, 0)[0]
                    dve.wait_ge(high_saved, splits + 1)
                    if kind == "W":
                        nc.vector.scalar_tensor_tensor(dst, src, WSCALE, high, ALU.mult, ALU.subtract).then_inc(task_saved, 1)
                    elif b16 is not None:
                        nc.vector.scalar_tensor_tensor(dst, src, b16, high, ALU.add, ALU.subtract).then_inc(task_saved, 1)
                    else:
                        nc.vector.tensor_tensor(dst, src, high, ALU.subtract).then_inc(task_saved, 1)
                elif kind == "V":
                    dve.wait_ge(task_ready, n + 1)
                    need(dve, v_moved[t[1]], DMA * batch)
                    nc.vector.tensor_copy(v_next[0:KP, t[1]], bank[0:KP, :]).then_inc(task_saved, 1)
                else:
                    q = t[1]
                    dve.wait_ge(task_ready, n + 1)
                    if q == 0:
                        dve.wait_ge(resid_ready, 2 * (batch + 1))
                    nc.vector.scalar_tensor_tensor(y[0:QP, q], bank[0:QP, :], 1.0 / (WSCALE * WSCALE), resid[0:QP, q],
                                                   ALU.mult, ALU.add).then_inc(task_saved, 1)
                    dve.wait_ge(task_saved, n + 1)
                    nc.vector.bn_stats(stats[0:QP, q], y[0:QP, q]).then_inc(stats_ready, 1)

            def mean_of(q):
                nc.vector.bn_aggr(mean_var[0:QP, q], stats[0:QP, q]).then_inc(mean_ready, 1)

            def center(q, batch):
                dve.wait_ge(rstd_ready, 2 * batch + q + 1)
                nc.vector.tensor_scalar(y[0:QP, q], y[0:QP, q], mean_var[0:QP, q, 0:1], rstd[0:QP, q:q + 1],
                                        ALU.subtract, ALU.mult).then_inc(centered, 1)

            def gamma_beta(q, batch):
                dve.wait_ge(centered, 2 * batch + q + 1)
                nc.vector.tensor_tensor(y[0:QP, q], y[0:QP, q], rows["gamma"][0:QP], ALU.mult).then_inc(last_scaled, 1)
                dve.wait_ge(last_scaled, 1)
                nc.vector.tensor_tensor(y[0:QP, q], y[0:QP, q], rows["beta"][0:QP], ALU.add).then_inc(last_ready, 1)

            def row_max(s, T):
                g, h, q = s // UNIT, s % UNIT // 2, s % 2
                for c in range(2):
                    dve.wait_ge(scores_ready, 2 * T + c + 1)
                    nc.vector.tensor_reduce(top_halves[0:QP, g % 2, q, h, c:c + 1], ps_scores[0:QP, BANK[2 * s + c], 0:KH],
                                            AX.X, ALU.max).then_inc(half_top_ready, 1)

            def unit_top(g, unit):
                dve.wait_ge(half_top_ready, 2 * UNIT * (unit + 1))
                need(dve, maxima_turned, unit - 1)
                nc.vector.tensor_reduce(top[0:QP, g % 2], top_halves[0:QP, g % 2], AX.X, ALU.max).then_inc(top_ready, 1)

            def invert_sums(u, half):
                cols = slice(QP * half, QP * half + QP)
                dve.wait_ge(attn_copied, u + 1)
                nc.vector.reciprocal(recip[:, cols], attn_sums[:, 1, cols]).then_inc(recip_ready, 1)

            def scale_attn(u):
                need(dve, attn_high_saved, u)
                need(dve, attn_low_saved, u)
                dve.wait_ge(recip_ready, 2 * (u + 1))
                nc.vector.tensor_tensor(attn[:], attn_sums[:, 0], recip[:], ALU.mult).then_inc(attn_scaled, 1)

            def sum_head(u, g, h):
                dve.wait_ge(probs_ready, PIECES * u + 3 * h + 3)
                nc.vector.tensor_reduce(head_sums[0:KP, g % 2, h, :], probsT[0:KP, g % 2, h].rearrange("p k q -> p q k"),
                                        AX.X, ALU.add).then_inc(last_sums_ready, 1)

            def attn_low(u, g):
                dve.wait_ge(attn_high_saved, u + 1)
                nc.vector.scalar_tensor_tensor(attn_parts[:, 1, g, :], attn[:], bias16["v"][:, g:g + 1],
                                               attn_parts[:, 0, g, :], ALU.add, ALU.subtract).then_inc(attn_low_saved, 1)

            splits = 0
            for n, t in enumerate(prologue):
                if n == PRO_BIASES:
                    dve.wait_ge(bias_loaded, 3 * DMA)
                    for w in "qkv":
                        nc.vector.tensor_scalar(bias16[w][:], bias[w][:], WSCALE, None, ALU.mult).then_inc(bias_ready, 1)
                    dve.wait_ge(bias_ready, 3)
                save_task(t, n, splits, pro_banks[n % PRO_BANKS], 0)
                splits += t[0] in SPLIT_KINDS
            row_max(0, 0)

            def iteration(b):
                tasks = iteration_tasks(b)
                before = tasks_before(b)
                for s in range(STEPS):
                    T = STEPS * b + s
                    g = s // UNIT
                    if has_output(b) and s - 2 in O_STEPS:
                        dve.wait_ge(stats_ready, 2 * (b - 1) + O_STEPS.index(s - 2) + 1)
                    if has_step(b, s + 1):
                        row_max((s + 1) % STEPS, T + 1)
                    if has_output(b) and s - 2 in O_STEPS:
                        mean_of(O_STEPS.index(s - 2))
                    if s % UNIT == UNIT - 1 and has_step(b, s):
                        unit_top(g, UNITS * b + g)
                    if s - 1 in tasks:
                        t, place, splits = tasks[s - 1]
                        save_task(t, before + place, splits_before(b) + splits, ps_task[:, place % 2], batch_of(t, s - 1, b))
                    for back, i, h in SUM_STEPS:
                        u = unit_before(b, g, back)
                        if u is not None and s % UNIT == i and vector_sums(HG * u + h):
                            sum_head(u, (g - back) % UNITS, h)
                    for half in range(2):
                        for u, _ in due(("invert", half), b, s):
                            invert_sums(u, half)
                    for u, _ in due("scale", b, s):
                        scale_attn(u)
                    for u, g_u in due("low", b, s):
                        attn_low(u, g_u)
                    last = isinstance(b, int) and b == B
                    wait_for_rstd = 4 if last else 3
                    if has_output(b) and s - wait_for_rstd in O_STEPS:
                        center(O_STEPS.index(s - wait_for_rstd), b - 1)
                        if last and s - wait_for_rstd == O_STEPS[1]:
                            dve.wait_ge(rows_loaded, 3 * DMA)
                            gamma_beta(1, b - 1)

            batches(dve, iteration)

        @block.gpsimd
        def _(pool):
            nc.gpsimd.memset(ident[:], 0.0).then_inc(ident_zero, 1)
            pool.wait_ge(ident_zero, 1)
            nc.gpsimd.affine_select(out=ident[:], in_=ident[:], compare_op=ALU.not_equal, fill=1.0, base=0,
                                    pattern=[[-1, P]], channel_multiplier=1).then_inc(ident_ready, 1)
            nc.gpsimd.memset(ones[:], 1.0).then_inc(ones_ready, 1)
            nc.gpsimd.memset(eps[:], 1e-5).then_inc(const_ready, 1)
            nc.gpsimd.memset(minus_half[:], -0.5).then_inc(const_ready, 1)
            pool.wait_ge(const_ready, 2)
            nc.gpsimd.memset(stacks[STACK_ROWS:STACK_ROWS + HG, :, :, Kc], 0.0).then_inc(pick_zero, 1)
            pool.wait_ge(pick_zero, 1)
            for g in range(UNITS):
                k_rows = stacks[STACK_ROWS:STACK_ROWS + HG, g, :, Kc]
                last = nc.gpsimd.affine_select(out=k_rows, in_=k_rows, compare_op=ALU.not_equal, fill=-MAX_SCALE,
                                               base=0, pattern=[[-1, HG], [0, NK]], channel_multiplier=1)
            last.then_inc(pick_ready, 1)
            pool.wait_ge(pick_ready, 1)

            def sum_head(u, g, h):
                n = sums_on_gpsimd(HG * u + h)
                pool.wait_ge(probs_ready, PIECES * u + 3 * h + 3)
                need(pool, head_sums_ready, n)
                nc.gpsimd.tensor_tensor(pair_sums[0:KP], probsT[0:KP, g % 2, h, 0:3, :], probsT[0:KP, g % 2, h, 3:6, :],
                                        ALU.add).then_inc(pair_sums_ready, 1)
                if h == 0:
                    need(pool, sums_ready, u - 1)
                pool.wait_ge(pair_sums_ready, n + 1)
                nc.gpsimd.tensor_tensor(head_sums[0:KP, g % 2, h, :], pair_sums[0:KP, 0], pair_sums[0:KP, 1],
                                        ALU.add).then_inc(two_sums_ready, 1)
                pool.wait_ge(two_sums_ready, n + 1)
                nc.gpsimd.tensor_tensor(head_sums[0:KP, g % 2, h, :], head_sums[0:KP, g % 2, h, :], pair_sums[0:KP, 2],
                                        ALU.add).then_inc(head_sums_ready, 1)

            def add_bo(q, batch):
                if q == 0:
                    pool.wait_ge(resid_loaded, DMA * (batch + 1))
                nc.gpsimd.tensor_tensor(resid[0:QP, q], resid[0:QP, q], rows["bo"][0:QP], ALU.add).then_inc(resid_ready, 1)

            def rstd_of(q, batch):
                pool.wait_ge(mean_ready, 2 * batch + q + 1)
                nc.gpsimd.tensor_tensor(var_eps[0:QP, q:q + 1], mean_var[0:QP, q, 1:2], eps[0:QP], ALU.add).then_inc(var_eps_ready, 1)
                pool.wait_ge(var_eps_ready, 2 * batch + q + 1)
                nc.gpsimd.tensor_tensor(rstd[0:QP, q:q + 1], var_eps[0:QP, q:q + 1], minus_half[0:QP], ALU.pow).then_inc(rstd_ready, 1)

            def times_gamma(q, batch):
                pool.wait_ge(centered, 2 * batch + q + 1)
                nc.gpsimd.tensor_tensor(y[0:QP, q], y[0:QP, q], rows["gamma"][0:QP], ALU.mult).then_inc(y_scaled, 1)

            def plus_beta(q, batch):
                pool.wait_ge(y_scaled, 2 * batch + q + 1)
                nc.gpsimd.tensor_tensor(y[0:QP, q], y[0:QP, q], rows["beta"][0:QP], ALU.add).then_inc(y_ready, 1)

            pool.wait_ge(rows_loaded, 3 * DMA)

            def iteration(b):
                for s in range(STEPS):
                    g = s // UNIT
                    for back, i, h in SUM_STEPS:
                        u = unit_before(b, g, back)
                        if u is not None and s % UNIT == i and not vector_sums(HG * u + h) and not is_last(u):
                            sum_head(u, (g - back) % UNITS, h)
                    if has_output(b):
                        for q in range(2):
                            if s == 9 + q:
                                add_bo(q, b - 1)
                            if s == O_STEPS[q] + 2:
                                rstd_of(q, b - 1)
                        for q in range(1 if isinstance(b, int) and b == B else 2):
                            if s == O_STEPS[q] + 4:
                                times_gamma(q, b - 1)
                            if s == O_STEPS[q] + 5:
                                plus_beta(q, b - 1)

            batches(pool, iteration)


_INS = ["x", "ctx_1024", "L0_xattn_Wq", "L0_xattn_bq", "L0_xattn_Wk", "L0_xattn_bk", "L0_xattn_Wv", "L0_xattn_bv",
        "L0_xattn_Wo", "L0_xattn_bo", "L0_xattn_gamma", "L0_xattn_beta"]


def kernel(**inputs):
    import numpy as np
    import concourse.bacc as bacc
    from concourse.bass_utils import run_bass_kernel_spmd

    nc = bacc.Bacc("TRN2", target_bir_lowering=False, num_devices=1)
    arrays, args = {}, []
    for name in _INS:
        a = np.ascontiguousarray(inputs[name])
        arrays[f"in_{name}"] = a
        args.append(nc.dram_tensor(f"in_{name}", a.shape, mybir.dt.from_np(a.dtype), kind="ExternalInput").ap())
    result = nc.dram_tensor("out_y", inputs["x"].shape, F32, kind="ExternalOutput").ap()
    build(nc, *args, result)
    r = run_bass_kernel_spmd(nc, [arrays], core_ids=[0])
    return r.results[0]["out_y"]
```
